# Optimizing a Trainium2 kernel written in Bass

```python
import numpy as np
import jax
import jax.numpy as jnp

def _softmax(x, axis=-1):
    return jax.nn.softmax(x, axis=axis)
def _gelu(x):
    return jax.nn.gelu(x, approximate=True)
def _silu(x):
    return jax.nn.silu(x)
def _sigmoid(x):
    return jax.nn.sigmoid(x)
def _layernorm(x, axis=-1, eps=1e-5):
    m = jnp.mean(x, axis=axis, keepdims=True)
    v = jnp.var(x, axis=axis, keepdims=True)
    return (x - m) / jnp.sqrt(v + eps)
def _scatter_add(tgt, idx, src, axis=0):
    return tgt.at[idx].add(src)
def _segment_sum(src, seg, n):
    return jax.ops.segment_sum(src, seg, n)

kernel_name = 'mk_adj_resnorm_d4_adj_256_bba13d'

def setup_inputs(seed: int = 0):
    np.random.seed(seed)
    _w = jnp.asarray
    def _rec_inputs():
        import jax
        import jax.numpy as jnp
        _gk = jax.random.key(seed)
        x = -0.0002928 + 1 * jax.random.normal(jax.random.fold_in(_gk, 1), (128, 128, 256), jnp.float32)
        _a = jax.random.bernoulli(jax.random.fold_in(_gk, 2), 0.03125, (128, 128, 128))
        _a = jnp.logical_or(_a, jnp.swapaxes(_a, -1, -2))
        _a = jnp.logical_or(_a, jnp.eye(128, dtype=bool))
        adj = _a.astype(jnp.int32)
        return x, adj
    x, adj = _rec_inputs()
    def _L0_gnn_setup():
        import jax, jax.numpy as jnp
        import numpy as np
        OUT = 256
        NUM_LAYERS = 3

        def _gru_cell(inp, h, w_ih, w_hh, b_ih, b_hh):
            gi = inp @ w_ih.T + b_ih
            gh = h @ w_hh.T + b_hh
            i_r, i_z, i_n = jnp.split(gi, 3, axis=-1)
            h_r, h_z, h_n = jnp.split(gh, 3, axis=-1)
            r = jax.nn.sigmoid(i_r + h_r)
            z = jax.nn.sigmoid(i_z + h_z)
            n = jnp.tanh(i_n + r * h_n)
            return (1.0 - z) * n + z * h
        key = jax.random.key(seed)
        ks = jax.random.split(key, 8)
        B, N, D = (32, 512, 256)
        x = jax.random.normal(ks[0], (B, N, D), dtype=jnp.float32)
        adj = jax.random.randint(ks[1], (B, N, N), 0, 2, dtype=jnp.int32)
        s = 1.0 / np.sqrt(OUT)
        weight = jax.random.uniform(ks[2], (NUM_LAYERS, OUT, OUT), jnp.float32, -s, s)
        w_ih = jax.random.uniform(ks[3], (3 * OUT, OUT), jnp.float32, -s, s)
        w_hh = jax.random.uniform(ks[4], (3 * OUT, OUT), jnp.float32, -s, s)
        b_ih = jax.random.uniform(ks[5], (3 * OUT,), jnp.float32, -s, s)
        b_hh = jax.random.uniform(ks[6], (3 * OUT,), jnp.float32, -s, s)
        return {'x': x, 'adj': adj, 'weight': weight, 'w_ih': w_ih, 'w_hh': w_hh, 'b_ih': b_ih, 'b_hh': b_hh}
    _L0_gnn_all = _L0_gnn_setup()
    _L0_gnn_in = {k: v for k, v in _L0_gnn_all.items() if k in ('weight', 'w_ih', 'w_hh', 'b_ih', 'b_hh', )}
    del _L0_gnn_all

    def _L1_gnn_setup():
        import jax, jax.numpy as jnp
        import numpy as np
        B, N, C_IN = (4, 2048, 256)
        H, C_HEAD = (8, 32)
        ALPHA = 0.2
        NEG_INF = -9000000000000000.0

        def glorot(key, shape, fan_in, fan_out):
            lim = jnp.sqrt(6.0 / (fan_in + fan_out))
            return jax.random.uniform(key, shape, jnp.float32, -lim, lim)
        key = jax.random.key(seed)
        k1, k2, k3, k4, k5 = jax.random.split(key, 5)
        x = jax.random.normal(k1, (B, N, C_IN), jnp.float32)
        G = jax.random.randint(k2, (B, N, N), 0, 2, jnp.int32)
        eye = jnp.eye(N, dtype=jnp.int32)[None]
        G = jnp.maximum(G, eye)
        proj_kernel = glorot(k3, (C_IN, H * C_HEAD), C_IN, H * C_HEAD)
        proj_bias = jnp.zeros((H * C_HEAD,), jnp.float32)
        attn_fst = glorot(k4, (H, C_HEAD), H, C_HEAD)
        attn_snd = glorot(k5, (H, C_HEAD), H, C_HEAD)
        return {'x': x, 'G': G, 'proj_kernel': proj_kernel, 'proj_bias': proj_bias, 'attn_fst': attn_fst, 'attn_snd': attn_snd}
    _L1_gnn_all = _L1_gnn_setup()
    _L1_gnn_in = {k: v for k, v in _L1_gnn_all.items() if k in ('proj_kernel', 'proj_bias', 'attn_fst', 'attn_snd', )}
    del _L1_gnn_all

    def _L2_gnn_setup():
        import jax, jax.numpy as jnp
        import numpy as np
        B, N, F_IN, F_OUT = (8, 2048, 256, 256)
        ALPHA = 0.2
        NEG_BIG = -9000000000000000.0
        key = jax.random.key(seed)
        k1, k2, k3, k4 = jax.random.split(key, 4)
        x = jax.random.normal(k1, (B, N, F_IN), dtype=jnp.float32)
        adj = jax.random.randint(k2, (B, N, N), 0, 2, dtype=jnp.int32)
        gain = 1.414
        lim_W = gain * np.sqrt(6.0 / (F_IN + F_OUT))
        W = jax.random.uniform(k3, (F_IN, F_OUT), dtype=jnp.float32, minval=-lim_W, maxval=lim_W)
        lim_a = gain * np.sqrt(6.0 / (2 * F_OUT + 1))
        a = jax.random.uniform(k4, (2 * F_OUT, 1), dtype=jnp.float32, minval=-lim_a, maxval=lim_a)
        return {'x': x, 'adj': adj, 'W': W, 'a': a}
    _L2_gnn_all = _L2_gnn_setup()
    _L2_gnn_in = {k: v for k, v in _L2_gnn_all.items() if k in ('W', 'a', )}
    del _L2_gnn_all

    def _L3_gnn_setup():
        import jax, jax.numpy as jnp
        import numpy as np
        ALPHA = 0.2
        NEG_INF = -9000000000000000.0
        key = jax.random.key(seed)
        k1, k2, k3, k4 = jax.random.split(key, 4)
        B, N, D = (8, 2048, 256)
        h = jax.random.normal(k1, (B, N, D), dtype=jnp.float32)
        adj = jax.random.randint(k2, (B, N, N), 0, 2, dtype=jnp.int32)
        W = jax.random.normal(k3, (D, D), dtype=jnp.float32) * (1.0 / np.sqrt(D))
        a = jax.random.normal(k4, (2 * D, 1), dtype=jnp.float32) * 0.05
        return {'h': h, 'adj': adj, 'W': W, 'a': a}
    _L3_gnn_all = _L3_gnn_setup()
    _L3_gnn_in = {k: v for k, v in _L3_gnn_all.items() if k in ('W', 'a', )}
    del _L3_gnn_all

    return {
        "x": x,
        "adj": adj,
        "L0_gnn_weight": _L0_gnn_in["weight"],
        "L0_gnn_w_ih": _L0_gnn_in["w_ih"],
        "L0_gnn_w_hh": _L0_gnn_in["w_hh"],
        "L0_gnn_b_ih": _L0_gnn_in["b_ih"],
        "L0_gnn_b_hh": _L0_gnn_in["b_hh"],
        "L1_gnn_proj_kernel": _L1_gnn_in["proj_kernel"],
        "L1_gnn_proj_bias": _L1_gnn_in["proj_bias"],
        "L1_gnn_attn_fst": _L1_gnn_in["attn_fst"],
        "L1_gnn_attn_snd": _L1_gnn_in["attn_snd"],
        "L2_gnn_W": _L2_gnn_in["W"],
        "L2_gnn_a": _L2_gnn_in["a"],
        "L3_gnn_W": _L3_gnn_in["W"],
        "L3_gnn_a": _L3_gnn_in["a"],
    }

def reference(x, adj, L0_gnn_weight, L0_gnn_w_ih, L0_gnn_w_hh, L0_gnn_b_ih, L0_gnn_b_hh, L1_gnn_proj_kernel, L1_gnn_proj_bias, L1_gnn_attn_fst, L1_gnn_attn_snd, L2_gnn_W, L2_gnn_a, L3_gnn_W, L3_gnn_a):
    import jax
    import jax.numpy as jnp
    def _L0_gnn_ref(x, adj, weight, w_ih, w_hh, b_ih, b_hh):
        import jax, jax.numpy as jnp
        import numpy as np
        OUT = 256
        NUM_LAYERS = 3

        def _gru_cell(inp, h, w_ih, w_hh, b_ih, b_hh):
            gi = inp @ w_ih.T + b_ih
            gh = h @ w_hh.T + b_hh
            i_r, i_z, i_n = jnp.split(gi, 3, axis=-1)
            h_r, h_z, h_n = jnp.split(gh, 3, axis=-1)
            r = jax.nn.sigmoid(i_r + h_r)
            z = jax.nn.sigmoid(i_z + h_z)
            n = jnp.tanh(i_n + r * h_n)
            return (1.0 - z) * n + z * h
        A = (adj != 0).astype(x.dtype)
        h = x
        L = weight.shape[0]
        for i in range(L):
            m = jnp.einsum('bnd,de->bne', h, weight[i])
            aggr = jnp.einsum('bst,bsd->btd', A, m)
            h = _gru_cell(aggr, h, w_ih, w_hh, b_ih, b_hh)
        return h

    def _L1_gnn_ref(x, G, proj_kernel, proj_bias, attn_fst, attn_snd):
        import jax, jax.numpy as jnp
        import numpy as np
        B, N, C_IN = (4, 2048, 256)
        H, C_HEAD = (8, 32)
        ALPHA = 0.2
        NEG_INF = -9000000000000000.0

        def glorot(key, shape, fan_in, fan_out):
            lim = jnp.sqrt(6.0 / (fan_in + fan_out))
            return jax.random.uniform(key, shape, jnp.float32, -lim, lim)
        b, n = (x.shape[0], x.shape[1])
        h = (x @ proj_kernel + proj_bias).reshape(b, n, H, C_HEAD)
        lf = jnp.einsum('bnhc,hc->bnh', h, attn_fst)
        ls = jnp.einsum('bnhc,hc->bnh', h, attn_snd)
        logit = lf[:, :, None, :] + ls[:, None, :, :]
        logit = jax.nn.leaky_relu(logit, negative_slope=ALPHA)
        logit = jnp.where(G[..., None] == 1, logit, NEG_INF)
        attn = jax.nn.softmax(logit, axis=2)
        out = jnp.einsum('bijh,bjhc->bihc', attn, h)
        return out.reshape(b, n, H * C_HEAD)

    def _L2_gnn_ref(x, adj, W, a):
        import jax, jax.numpy as jnp
        import numpy as np
        B, N, F_IN, F_OUT = (8, 2048, 256, 256)
        ALPHA = 0.2
        NEG_BIG = -9000000000000000.0
        h = jnp.einsum('bnf,fo->bno', x, W)
        a1 = a[:F_OUT, 0]
        a2 = a[F_OUT:, 0]
        s1 = h @ a1
        s2 = h @ a2
        e = jax.nn.leaky_relu(s1[:, :, None] + s2[:, None, :], negative_slope=ALPHA)
        att = jnp.where(adj > 0, e, jnp.float32(NEG_BIG))
        att = jax.nn.softmax(att, axis=1)
        h_prime = jnp.einsum('bij,bjo->bio', att, h)
        return jax.nn.elu(h_prime)

    def _L3_gnn_ref(h, adj, W, a):
        import jax, jax.numpy as jnp
        import numpy as np
        ALPHA = 0.2
        NEG_INF = -9000000000000000.0
        Wh = jnp.einsum('bnd,od->bno', h, W)
        D = Wh.shape[-1]
        a1, a2 = (a[:D, 0], a[D:, 0])
        s1 = Wh @ a1
        s2 = Wh @ a2
        e = jax.nn.leaky_relu(s1[:, :, None] + s2[:, None, :], negative_slope=ALPHA)
        e = jnp.where(adj > 0, e, NEG_INF)
        attention = jax.nn.softmax(e, axis=-1)
        h_prime = jnp.einsum('bij,bjd->bid', attention, Wh)
        return h_prime

    x = _layernorm(x + _L0_gnn_ref(x, adj, L0_gnn_weight, L0_gnn_w_ih, L0_gnn_w_hh, L0_gnn_b_ih, L0_gnn_b_hh), axis=-1)
    x = _layernorm(x + _L1_gnn_ref(x, adj, L1_gnn_proj_kernel, L1_gnn_proj_bias, L1_gnn_attn_fst, L1_gnn_attn_snd), axis=-1)
    x = _layernorm(x + _L2_gnn_ref(x, adj, L2_gnn_W, L2_gnn_a), axis=-1)
    x = _layernorm(x + _L3_gnn_ref(x, adj, L3_gnn_W, L3_gnn_a), axis=-1)
    return x


_drawn_inputs = setup_inputs


def setup_inputs(seed=0):
    import zlib

    import numpy as np

    out = dict(_drawn_inputs(seed))
    spreads = {'L1_gnn_proj_bias': (0.0, 0.1)}
    factors = {}
    for name, (base, spread) in spreads.items():
        noise = np.random.default_rng([zlib.crc32(name.encode()), seed]).standard_normal(out[name].shape)
        drawn = base * np.exp(spread * noise) if base else spread * noise
        out[name] = jnp.asarray(drawn.astype(out[name].dtype))
    for name, factor in factors.items():
        out[name] = (out[name] * factor).astype(out[name].dtype)
    return out
```

```python
from contextlib import ExitStack

import concourse.bass as bass
from concourse import mybir

ALU = mybir.AluOpType
ACT = mybir.ActivationFunctionType
AX = mybir.AxisListType
F32 = mybir.dt.float32
F32R = mybir.dt.float32r
BF16 = mybir.dt.bfloat16
I32 = mybir.dt.int32

P = 128
GS = 2
NS = 2
TOK = GS * P
MASKED = -9.0e15
SLOPE = 0.2
EPS = 1e-5
SLOTS = 6

CONTENT = [(1, "T", 0), (1, "P", 0), (1, "P", 1), (1, "R", 0), (1, "X", 0), (1, "X", 1), (1, "Y", 0),
           (1, "X", 2), (1, "Y", 1), (1, "A", 0), (1, "X", 3), (1, "Y", 2), (1, "Y", 3), (1, "A", 1),
           (2, "T", 0), (2, "P", 0), (2, "P", 1), (2, "R", 0), (2, "X", 0), (2, "A", 0),
           (3, "T", 0), (3, "P", 0), (3, "P", 1), (3, "R", 0), (3, "X", 0), (3, "Y", 0), (3, "A", 0)]
NJ = len(CONTENT)
POS = {c: j for j, c in enumerate(CONTENT)}


def make_schedule():
    order = [("begin", 0), ("init", 0)]
    gaps = list(range(14)) + [None] + list(range(14, 20)) + [None] + list(range(20, 27))
    second, third = [], []

    def gap():
        for j in third:
            order.append(("att3", j))
        for j in second:
            order.append(("att2", j))
        third[:] = second
        second[:] = [gaps.pop(0)] if gaps else []
        if second == [None]:
            second.clear()
        for j in second:
            order.append(("att", j))

    for n in range(SLOTS):
        order.append(("agg", n))
        gap()
        order.append(("gates_h", (n, 0)))
        if n:
            order.append(("gru", (n - 1, 1)))
        order.append(("gates_u", (n, 0)))
        if n:
            order.append(("turn", n - 1))
        else:
            order.append(("init", 1))
        gap()
        order.append(("gates_h", (n, 1)))
        order.append(("gru", (n, 0)))
        gap()
        order.append(("gates_u", (n, 1)))
        gap()
    order.append(("gru", (SLOTS - 1, 1)))
    while gaps or second or third:
        gap()
    order.append(("turn", SLOTS - 1))
    order.append(("end", 0))
    return order


def graph_layers(nc, x, adj, weight, w_ih, w_hh, b_ih, b_hh, proj, proj_b, a_fst, a_snd, W2, a2, W3, a3, out):
    B, N, D = x.shape
    L = weight.shape[0]
    H, C = a_fst.shape
    G3 = 3 * D
    KC = D // P
    NB = B // (GS * NS)
    L1C, L2C = D + 2 * H, D + 2
    assert (N, D, L, H * C) == (P, 256, 3, D)
    order = make_schedule()

    with ExitStack() as ctx:
        def sb(name, shape, dt=F32):
            return ctx.enter_context(nc.sbuf_tensor(name, shape, dt))

        def psum(name):
            return ctx.enter_context(nc.psum_tensor(name, [P, 512], F32))

        def sem(name):
            return ctx.enter_context(nc.semaphore(name))

        def sems(name, n=NS):
            return [sem(f"{name}_{i}") for i in range(n)]

        gates_rz = [psum(f"gates_rz_{c}") for c in range(KC)]
        gates_ih = [psum(f"gates_ih_{c}") for c in range(KC)]
        agg_bank = psum("agg_bank")
        turn_bank = psum("turn_bank")
        att_bank = [psum(f"att_bank_{s}") for s in range(NS)]

        whh_hi, whh_lo = (sb(n, [P, KC, G3], F32R) for n in ("whh_hi", "whh_lo"))
        wc_hi, wc_lo = (sb(n, [P, L, KC, G3], F32R) for n in ("wc_hi", "wc_lo"))
        p1_hi, p1_lo = (sb(n, [P, KC, L1C], F32R) for n in ("p1_hi", "p1_lo"))
        p2_hi, p2_lo = (sb(n, [P, KC, L2C], F32R) for n in ("p2_hi", "p2_lo"))
        p3_hi, p3_lo = (sb(n, [P, KC, L2C], F32R) for n in ("p3_hi", "p3_lo"))
        bias1 = sb("bias1", [P, L1C])
        bi, bh, bsum, half_b, half_bh = (sb(n, [P, 6]) for n in ("bi", "bh", "bsum", "half_b", "half_bh"))
        ident = sb("ident", [P, P])
        ident_b = sb("ident_b", [P, P], BF16)
        pick16 = sb("pick16", [48, 16])
        pick2 = sb("pick2", [6, 2])
        sel16 = sb("sel16", [48, 16, P], BF16)
        sel2 = sb("sel2", [6, 2, P], BF16)
        minus_half = sb("minus_half", [P, GS])

        x_in = [sb(f"x_in_{s}", [P, GS, D]) for s in range(NS)]
        adj_in = [sb(f"adj_in_{s}", [P, GS, P], I32) for s in range(NS)]
        x_keep = [sb(f"x_keep_{s}", [P, GS, D]) for s in range(NS)]
        edges = [sb(f"edges_{s}", [P, GS, P]) for s in range(NS)]
        neg1_next = [sb(f"neg1_next_{s}", [P, GS, P], BF16) for s in range(NS)]
        neg3_next = [sb(f"neg3_next_{s}", [P, GS, P], BF16) for s in range(NS)]
        h_feat = [sb(f"h_feat_{s}", [P, KC, TOK]) for s in range(NS)]
        h_hi = [sb(f"h_hi_{s}", [P, KC, TOK], F32R) for s in range(NS)]
        h_lo = [sb(f"h_lo_{s}", [P, KC, TOK], F32R) for s in range(NS)]
        h_node = [sb(f"h_node_{s}", [P, GS, D]) for s in range(NS)]
        u_hi, u_lo = (sb(n, [P, KC, TOK], F32R) for n in ("u_hi", "u_lo"))
        tr, tz, hn, pre, nn, dd = ([sb(f"{n}_{c}", [P, TOK]) for c in range(KC)]
                                   for n in ("tr", "tz", "hn", "pre", "nn", "dd"))
        y = [sb(f"y_{s}", [P, GS, D]) for s in range(NS)]
        y0 = [sb(f"y0_{s}", [P, GS, D]) for s in range(NS)]
        xn = [sb(f"xn_{s}", [P, GS, D]) for s in range(NS)]
        xT_hi = [sb(f"xT_hi_{s}", [P, KC, TOK], F32R) for s in range(NS)]
        xT_lo = [sb(f"xT_lo_{s}", [P, KC, TOK], F32R) for s in range(NS)]
        neg1 = [sb(f"neg1_{s}", [P, GS, P], BF16) for s in range(NS)]
        neg3 = [sb(f"neg3_{s}", [P, GS, P], BF16) for s in range(NS)]
        h1 = [sb(f"h1_{s}", [P, GS, H, C + 1]) for s in range(NS)]
        h2 = [sb(f"h2_{s}", [P, GS, L2C]) for s in range(NS)]
        terms = [sb(f"terms_{s}", [P, GS, 2 * H]) for s in range(NS)]
        rest = [sb(f"rest_{s}", [P, GS, 2 * H]) for s in range(NS)]
        parts = [sb(f"parts_{s}", [P, GS, 3, 2 * H], BF16) for s in range(NS)]
        parts2 = [sb(f"parts2_{s}", [P, GS, 3, 2], BF16) for s in range(NS)]
        rows = [sb(f"rows_{s}", [48, GS, P], BF16) for s in range(NS)]
        prob = [[sb(f"prob_{s}_{i}", [P, 4, P]) for i in range(2)] for s in range(NS)]
        top = [[sb(f"top_{s}_{i}", [P, 4]) for i in range(2)] for s in range(NS)]
        mtop = [[sb(f"mtop_{s}_{i}", [P, 4]) for i in range(2)] for s in range(NS)]
        probT = [sb(f"probT_{s}", [P, H, P]) for s in range(NS)]
        zsum = [sb(f"zsum_{s}", [P, GS]) for s in range(NS)]
        rz = [sb(f"rz_{s}", [P, H]) for s in range(NS)]
        below = [sb(f"below_{s}", [P, GS, D]) for s in range(NS)]
        stats = [sb(f"stats_{s}", [P, GS, 6]) for s in range(NS)]
        mv = [sb(f"mv_{s}", [P, GS, 2]) for s in range(NS)]
        veps = [sb(f"veps_{s}", [P, GS]) for s in range(NS)]
        rstd = [sb(f"rstd_{s}", [P, GS]) for s in range(NS)]
        result = [sb(f"result_{s}", [P, GS, D]) for s in range(NS)]
        raw_ih, raw_hh = (sb(n, [P, 6, D]) for n in ("raw_ih", "raw_hh"))
        raw_w = sb("raw_w", [P, L, KC, D])
        raw_p1, raw_p2, raw_p3, p1T, p2T = result[0], result[1], y[0], below[0], below[1]
        wihT = sb("wihT", [P, KC, G3])
        wT = sb("wT", [P, L, KC, D])
        a_block = sb("a_block", [P, KC, 2 * H])
        a2_cols, a3_cols = (sb(n, [P, 2, KC]) for n in ("a2_cols", "a3_cols"))
        b_col = sb("b_col", [P, KC])
        b_wide = sb("b_wide", [P, KC, P])

        ident_zero, ident_ready, block_zero, half_ready = (sem(n) for n in ("ident_zero", "ident_ready", "block_zero", "half_ready"))
        weights_in, vectors_in = sem("weights_in"), sem("vectors_in")
        setup_filled, setup_drained, setup_dve, setup_hi, setup_done = (
            sem(n) for n in ("setup_filled", "setup_drained", "setup_dve", "setup_hi", "setup_done"))
        x_loaded, adj_loaded, x_kept, masks_ready = (sems(n) for n in ("x_loaded", "adj_loaded", "x_kept", "masks_ready"))
        gates_filled, h_used, r_hn_ready, z_ready, q_ready, pre_ready, n_ready, d_ready, e_ready, h_ready = (
            sems(n, KC) for n in ("gates_filled", "h_used", "r_hn_ready", "z_ready", "q_ready", "pre_ready",
                                  "n_ready", "d_ready", "e_ready", "h_ready"))
        h_hi_ready, h_lo_ready = sems("h_hi_ready"), sems("h_lo_ready")
        agg_filled, u_hi_ready, u_ready = sem("agg_filled"), sem("u_hi_ready"), sem("u_ready")
        turn_filled, turn_drained = sem("turn_filled"), sem("turn_drained")
        neg_moved = sems("neg_moved")
        att_filled, att_drained, xT_hi_ready, cut_done, rest_done, parts_ready = (
            sems(n) for n in ("att_filled", "att_drained", "xT_hi_ready", "cut_done", "rest_done", "parts_ready"))
        scaled_ready, top_ready, mtop_ready, shifted, summed, prob_ready, rz_ready = (
            sems(n) for n in ("scaled_ready", "top_ready", "mtop_ready", "shifted", "summed", "prob_ready", "rz_ready"))
        below_ready, elu_ready, y_ready, stats_ready, mv_ready, veps_ready, rstd_ready, xn_ready, result_ready, stored = (
            sems(n) for n in ("below_ready", "elu_ready", "y_ready", "stats_ready", "mv_ready", "veps_ready", "rstd_ready",
                              "xn_ready", "result_ready", "stored"))

        def nth(k, per, i):
            return k * per + (i + 1)

        x_v = x.rearrange("(k s g) n d -> k s n g d", s=NS, g=GS)
        adj_v = adj.rearrange("(k s g) n m -> k s n g m", s=NS, g=GS)
        out_v = out.rearrange("(k s g) n d -> k s n g d", s=NS, g=GS)

        TURN = 8

        def bank3(bank, a):
            return bank[:].rearrange("p (a b) -> p a b", a=a)

        panels = [("turn", "ih", i) for i in range(3)] + [("turn", "w", i) for i in range(L)]
        panels += [("turn", "hh", i) for i in range(3)] + [("turn", m, 0) for m in ("p1", "p2", "p3")]
        panels += [("fold", i, (dc, nh)) for i in range(L) for dc in range(KC) for nh in range(2)]
        panels += [("terms", m, dc) for m in ("p1", "p2", "p3") for dc in range(KC)] + [("terms", "bias", 0)]
        setup_bank = [agg_bank, turn_bank]
        N_WEIGHTS, N_VECTORS = 6, 6 + 2 * H

        block = ctx.enter_context(nc.Block())

        @block.sync
        def _(sp):
            def load(k):
                for s in range(NS):
                    if not (isinstance(k, int) and k == 0):
                        sp.wait_ge(x_kept[s], k)
                        sp.nop(nofuse=True)
                        sp.wait_ge(masks_ready[s], k * 3)
                        sp.nop(nofuse=True)
                    sp.dma_start(x_in[s][:], x_v[k, s]).then_inc(x_loaded[s], 16)
                    sp.dma_start(adj_in[s][:], adj_v[k, s]).then_inc(adj_loaded[s], 16)

            def store(kg):
                for s in range(NS):
                    sp.wait_ge(result_ready[s], nth(kg, 1, 0))
                    sp.nop(nofuse=True)
                    sp.dma_start(out_v[kg, s], result[s][:]).then_inc(stored[s], 16)

            sp.dma_start(raw_ih[:], w_ih.rearrange("(c p) d -> p c d", p=P)).then_inc(weights_in, 16)
            sp.dma_start(raw_w[:], weight.rearrange("l (c p) d -> p l c d", p=P)).then_inc(weights_in, 16)
            sp.dma_start(raw_hh[:], w_hh.rearrange("(c p) d -> p c d", p=P)).then_inc(weights_in, 16)
            for raw, src in ((raw_p1, proj), (raw_p2, W2), (raw_p3, W3)):
                sp.dma_start(raw[:], src.rearrange("(c p) d -> p c d", p=P)).then_inc(weights_in, 16)
            load(0)
            load(1)
            with sp.Fori(1, NB - 1) as k:
                load(k + 1)
                store(k - 1)
            store(NB - 2)
            store(NB - 1)
            for s in range(NS):
                sp.wait_ge(stored[s], 16 * NB + 1)

        @block.gpsimd
        def _(pool):
            pool.memset(ident[:], 0.0).then_inc(ident_zero, 1)
            pool.wait_ge(ident_zero, 1)
            pool.affine_select(out=ident[:], in_=ident[:], compare_op=ALU.not_equal, fill=1.0, base=0,
                               pattern=[[-1, P]], channel_multiplier=1).then_inc(ident_ready, 1)
            pool.memset(minus_half[:], -0.5).then_inc(half_ready, 1)
            pool.wait_ge(half_ready, 1)
            for s in range(NS):
                pool.memset(rstd[s][:], 1.0).then_inc(stored[s], 1)

            def body(k, gru, att):
                kg = k - 1
                for what, arg in order:
                    if what == "begin" and gru:
                        for s in range(NS):
                            pool.wait_ge(x_loaded[s], 16 * (k + 1))
                            if att:
                                pool.wait_ge(turn_drained, nth(kg, TURN, SLOTS + s))
                            pool.nop(nofuse=True)
                            pool.tensor_copy(x_keep[s][:], x_in[s][:]).then_inc(x_kept[s], 1)
                    if what == "begin" and att:
                        for s in range(NS):
                            inv_std(s, kg, 0)
                    if what == "init" and gru:
                        s = arg
                        pool.wait_ge(turn_drained, nth(k, TURN, s))
                        pool.nop(nofuse=True)
                        pool.tensor_copy(h_hi[s][:], h_feat[s][:]).then_inc(h_hi_ready[s], 1)
                        pool.wait_ge(h_hi_ready[s], nth(k, 5, 0))
                        pool.tensor_tensor(h_lo[s][:], h_feat[s][:], h_hi[s][:].bitcast(F32),
                                           ALU.subtract).then_inc(h_lo_ready[s], 1)
                    if what == "gru" and gru:
                        n, c = arg
                        s = n % 2
                        pool.wait_ge(n_ready[c], nth(k, 6, n))
                        pool.tensor_tensor(dd[c][:], h_feat[s][:, c, :], nn[c][:], ALU.subtract).then_inc(d_ready[c], 1)
                        if n < SLOTS - NS:
                            i = 1 + 2 * (n // 2) + c
                            pool.wait_ge(h_used[1], nth(k, 6, n))
                            pool.wait_ge(h_ready[c], nth(k, 6, n))
                            pool.nop(nofuse=True)
                            pool.tensor_copy(h_hi[s][:, c, :], h_feat[s][:, c, :]).then_inc(h_hi_ready[s], 1)
                            pool.wait_ge(h_hi_ready[s], nth(k, 5, i))
                            pool.tensor_tensor(h_lo[s][:, c, :], h_feat[s][:, c, :], h_hi[s][:, c, :].bitcast(F32),
                                               ALU.subtract).then_inc(h_lo_ready[s], 1)
                    if what == "att" and att:
                        layer, kind, u = CONTENT[arg]
                        for s in range(NS):
                            if kind == "P" and u == GS - 1:
                                cut_terms(s, kg, layer)
                            if kind == "A" and (layer, u) in ((1, 1), (3, 0)):
                                inv_std(s, kg, layer)
                    if what == "att2" and att:
                        layer, kind, u = CONTENT[arg]
                        for s in range(NS):
                            if kind == "X" and layer == 1:
                                pool.wait_ge(mtop_ready[s], nth(kg, 6, u))
                                pool.wait_ge(att_drained[s], nth(kg, NJ, arg))
                                e = prob[s][u % 2][:]
                                m = mtop[s][u % 2][:, 0:4].unsqueeze(2).to_broadcast([P, 4, P])
                                pool.tensor_tensor(e, e, m, ALU.subtract).then_inc(shifted[s], 1)
                            if kind == "A" and layer == 2:
                                inv_std(s, kg, layer)
                    if what == "end" and gru:
                        for s in range(NS):
                            pool.wait_ge(masks_ready[s], nth(k, 3, 2))
                            if att:
                                pool.wait_ge(att_filled[s], nth(kg, NJ, POS[3, "X", 0]))
                            pool.nop(nofuse=True)
                            pool.tensor_copy(neg1[s][:], neg1_next[s][:]).then_inc(neg_moved[s], 1)
                            pool.nop(nofuse=True)
                            pool.tensor_copy(neg3[s][:], neg3_next[s][:]).then_inc(neg_moved[s], 1)

            def inv_std(s, kg, i):
                pool.wait_ge(veps_ready[s], nth(kg, 4, i))
                pool.tensor_tensor(rstd[s][:], veps[s][:], minus_half[:], ALU.pow).then_inc(rstd_ready[s], 1)

            def cut_terms(s, kg, layer):
                pool.wait_ge(att_drained[s], nth(kg, NJ, POS[layer, "P", GS - 1]))
                w = 2 * H if layer == 1 else 2
                src = terms[s][:] if layer == 1 else h2[s][:, :, D:L2C]
                to = parts[s] if layer == 1 else parts2[s]
                left = rest[s][:, :, 0:w]
                pool.nop(nofuse=True)
                pool.tensor_copy(to[:, :, 0, :], src).then_inc(cut_done[s], 1)
                pool.wait_ge(cut_done[s], nth(kg, 6, 2 * (layer - 1)))
                pool.tensor_tensor(left, src, to[:, :, 0, :], ALU.subtract).then_inc(rest_done[s], 1)
                pool.wait_ge(rest_done[s], nth(kg, 3, layer - 1))
                pool.nop(nofuse=True)
                pool.tensor_copy(to[:, :, 1, :], left).then_inc(cut_done[s], 1)
                pool.wait_ge(cut_done[s], nth(kg, 6, 2 * (layer - 1) + 1))
                pool.tensor_tensor(to[:, :, 2, :], left, to[:, :, 1, :], ALU.subtract).then_inc(parts_ready[s], 1)

            body(0, True, False)
            with pool.Fori(1, NB) as k:
                body(k, True, True)
            body(NB, False, True)

        @block.tensor
        def _(pe):
            def three_pass(o, w_hi, w_lo, x_hi, x_lo, start, stop):
                pe.matmul(o, w_hi, x_hi, start=start, stop=False, skip_group_check=True)
                pe.matmul(o, w_hi, x_lo, start=False, stop=False, skip_group_check=True)
                return pe.matmul(o, w_lo, x_hi, start=False, stop=stop, skip_group_check=True)

            pe.wait_ge(ident_ready, 1)
            pe.wait_ge(weights_in, 16 * N_WEIGHTS)
            raws = {"ih": raw_ih, "hh": raw_hh, "p1": raw_p1, "p2": raw_p2, "p3": raw_p3}
            for q, (what, m, i) in enumerate(panels):
                bank = setup_bank[q % 2]
                if q >= 2:
                    pe.wait_ge(setup_drained, q - 1)
                if what == "turn":
                    for f in range(4):
                        if m in ("ih", "hh"):
                            kc, c = divmod(4 * i + f, 6)
                            src = raws[m][:, c, kc * P:(kc + 1) * P]
                        elif m == "w":
                            kc, c = divmod(f, KC)
                            src = raw_w[:, i, c, kc * P:(kc + 1) * P]
                        else:
                            kc, c = divmod(f, KC)
                            src = raws[m][:, c, kc * P:(kc + 1) * P]
                        last = pe.transpose(bank[:, f * P:(f + 1) * P], src, ident[:])
                elif what == "fold":
                    dc, nh = i
                    n0, n1 = ((0, 512), (512, G3))[nh]
                    for kc in range(KC):
                        last = pe.matmul(bank[:, 0:n1 - n0], wT[:, m, kc, dc * P:(dc + 1) * P],
                                         wihT[:, kc, n0:n1], start=(kc == 0), stop=(kc == KC - 1))
                else:
                    if m == "p1" and i == 0:
                        pe.wait_ge(vectors_in, 16 * N_VECTORS)
                        pe.wait_ge(setup_dve, 5)
                    w = 2 * H if m in ("p1", "bias") else 2
                    for kc in range(KC):
                        lhs = {"p1": p1T, "p2": p2T, "p3": raw_p3}.get(m)
                        lhs = b_wide[:, kc, :] if m == "bias" else lhs[:, kc, i * P:(i + 1) * P]
                        rhs = {"p2": a2_cols, "p3": a3_cols}.get(m)
                        rhs = a_block[:, kc, :] if m in ("p1", "bias") else rhs[:, :, kc]
                        last = pe.matmul(bank[:, 0:w], lhs, rhs, start=(kc == 0), stop=(kc == KC - 1))
                last.then_inc(setup_filled, 1)
            pe.wait_ge(setup_done, 1)

            def turn(bank, src):
                o = bank[:].rearrange("p (c t) -> p c t", c=KC)
                for c in range(KC):
                    for g in range(GS):
                        last = pe.transpose(o[:, c, g * P:(g + 1) * P], src[:, g, c * P:(c + 1) * P], ident[:])
                return last

            def body(k, gru, att):
                kg = k - 1
                for what, arg in order:
                    if what == "init" and gru:
                        s = arg
                        pe.wait_ge(x_kept[s], nth(k, 1, 0))
                        pe.wait_ge(turn_drained, k * TURN + s)
                        turn(turn_bank, x_keep[s]).then_inc(turn_filled, 1)
                    if what == "agg" and gru:
                        n, s = arg, arg % 2
                        if n < NS:
                            pe.wait_ge(x_kept[s], nth(k, 1, 0))
                            pe.wait_ge(masks_ready[s], nth(k, 3, 0))
                            node = x_keep[s]
                        else:
                            pe.wait_ge(turn_drained, nth(k, TURN, n))
                            node = h_node[s]
                        pe.wait_ge(u_ready, k * 6 + n)
                        o = bank3(agg_bank, KC)
                        for c in range(KC):
                            for g in range(GS):
                                last = pe.matmul(o[:, c, g * P:(g + 1) * P], node[:, g, c * P:(c + 1) * P],
                                                 edges[s][:, g, :], start=True, stop=True)
                        last.then_inc(agg_filled, 1)
                    if what == "gates_h" and gru:
                        n, c = arg
                        s = n % 2
                        pe.wait_ge(h_lo_ready[s], nth(k, 5, 2 * (n // 2)))
                        pe.wait_ge(pre_ready[c], k * 6 + n)
                        pe.wait_ge(z_ready[c], k * 6 + n)
                        for bank, half, gate in ((gates_rz[c], 0, 0), (gates_rz[c], 1, 1), (gates_ih[c], 1, 2)):
                            col = gate * D + c * P
                            for kc in range(KC):
                                last = three_pass(bank3(bank, 2)[:, half, :], whh_hi[:, kc, col:col + P],
                                                  whh_lo[:, kc, col:col + P], h_hi[s][:, kc, :], h_lo[s][:, kc, :],
                                                  start=(kc == 0 and gate != 1), stop=False)
                        last.then_inc(h_used[c], 1)
                    if what == "gates_u" and gru:
                        n, c = arg
                        it = n // 2
                        pe.wait_ge(u_ready, nth(k, 6, n))
                        for bank, half, gate in ((gates_rz[c], 0, 0), (gates_rz[c], 1, 1), (gates_ih[c], 0, 2)):
                            col = gate * D + c * P
                            for kc in range(KC):
                                last = three_pass(bank3(bank, 2)[:, half, :], wc_hi[:, it, kc, col:col + P],
                                                  wc_lo[:, it, kc, col:col + P], u_hi[:, kc, :], u_lo[:, kc, :],
                                                  start=False, stop=(kc == KC - 1))
                        last.then_inc(gates_filled[c], 1)
                    if what == "turn" and gru:
                        n, s = arg, arg % 2
                        pe.wait_ge(turn_drained, k * TURN + n + 2)
                        for c in range(KC):
                            pe.wait_ge(h_ready[c], nth(k, 6, n))
                        o = bank3(turn_bank, GS)
                        for g in range(GS):
                            for c in range(KC):
                                last = pe.transpose(o[:, g, c * P:(c + 1) * P], h_feat[s][:, c, g * P:(g + 1) * P], ident[:])
                        last.then_inc(turn_filled, 1)
                    if what == "att" and att:
                        layer, kind, u = CONTENT[arg]
                        for s in range(NS):
                            if arg:
                                pe.wait_ge(att_drained[s], kg * NJ + arg)
                            content(s, kg, layer, kind, u).then_inc(att_filled[s], 1)

            def content(s, kg, layer, kind, u):
                bank = att_bank[s]
                if kind == "T":
                    pe.wait_ge(xn_ready[s], nth(kg, 3, layer - 1))
                    return turn(bank, xn[s])
                if kind == "P":
                    w_hi, w_lo, w = {1: (p1_hi, p1_lo, L1C), 2: (p2_hi, p2_lo, L2C), 3: (p3_hi, p3_lo, L2C)}[layer]
                    for kc in range(KC):
                        a_hi, a_lo = (t[s][:, kc, u * P:(u + 1) * P] for t in (xT_hi, xT_lo))
                        last = three_pass(bank[:, 0:w], a_hi, a_lo, w_hi[:, kc, :], w_lo[:, kc, :],
                                          start=(kc == 0), stop=(kc == KC - 1))
                    return last
                if kind == "R":
                    pe.wait_ge(parts_ready[s], nth(kg, 3, layer - 1))
                    pe.nop(nofuse=True)
                    w = 48 if layer == 1 else 6
                    src = parts[s] if layer == 1 else parts2[s]
                    o = bank[0:w, 0:P].bitcast(BF16).rearrange("r (g i) -> r g i", g=GS)
                    for g in range(GS):
                        last = pe.transpose(o[:, g, :], src[:, g].rearrange("p a b -> p (a b)"), ident_b[:])
                    return last
                if kind == "X" and layer == 1:
                    pe.wait_ge(neg_moved[s], nth(kg, 2, 1))
                    g, half = divmod(u, 2)
                    row = rows[s][0:48, g, :]
                    pe.matmul(bank[:], ident_b[:], neg1[s][:, g, :].unsqueeze(1).to_broadcast([P, 4, P]),
                              start=True, stop=False, skip_group_check=True)
                    pe.matmul(bank[:], row, sel16[:, 4 * half:4 * half + 4, :].rearrange("r a b -> r (a b)"),
                              start=False, stop=False, skip_group_check=True)
                    for q in range(4):
                        last = pe.matmul(bank[:, q * P:(q + 1) * P], sel16[:, H + 4 * half + q, :], row,
                                         start=False, stop=(q == 3), skip_group_check=True)
                    return last
                if kind == "X":
                    pe.wait_ge(neg_moved[s], nth(kg, 2, 1))
                    for g in range(GS):
                        o = bank[:, g * P:(g + 1) * P]
                        row = rows[s][0:6, g, :]
                        if layer == 2:
                            pe.matmul(o, neg3[s][:, g, :], ident_b[:], start=(g == 0), stop=False, skip_group_check=True)
                        else:
                            pe.matmul(o, ident_b[:], neg3[s][:, g, :], start=(g == 0), stop=False, skip_group_check=True)
                        free, part = (0, 1) if layer == 2 else (1, 0)
                        pe.matmul(o, sel2[:, free, :], row, start=False, stop=False, skip_group_check=True)
                        last = pe.matmul(o, row, sel2[:, part, :], start=False, stop=(g == 1), skip_group_check=True)
                    return last
                if kind == "Y":
                    if layer == 1:
                        pe.wait_ge(prob_ready[s], nth(kg, 5, u))
                        for q in range(4):
                            last = pe.transpose(bank[:, q * P:(q + 1) * P], prob[s][u % 2][:, q, :], ident[:])
                    else:
                        pe.wait_ge(summed[s], nth(kg, 2, 1))
                        for g in range(GS):
                            last = pe.transpose(bank[:, g * P:(g + 1) * P], prob[s][0][:, g, :], ident[:])
                    return last
                if layer == 1:
                    for q in range(H):
                        last = pe.matmul(bank[:, q * (C + 1):(q + 1) * (C + 1)], probT[s][:, q, :],
                                         h1[s][:, u, q, :], start=True, stop=True)
                    return last
                if layer == 2:
                    pe.wait_ge(prob_ready[s], nth(kg, 5, 4))
                for g in range(GS):
                    lhs = prob[s][0][:, g, :] if layer == 2 else probT[s][:, g, :]
                    last = pe.matmul(bank[:, g * D:(g + 1) * D], lhs, h2[s][:, g, 0:D], start=True, stop=True)
                return last

            body(0, True, False)
            with pe.Fori(1, NB) as k:
                body(k, True, True)
            body(NB, False, True)

        @block.scalar
        def _(act):
            with nc.allow_non_contiguous_dma(reason="vectors of the setup, once"):
                act.dma_start(bi[:], b_ih.rearrange("(c p) -> p c", p=P)).then_inc(vectors_in, 16)
                act.dma_start(bh[:], b_hh.rearrange("(c p) -> p c", p=P)).then_inc(vectors_in, 16)
                act.dma_start(b_col[:], proj_b.rearrange("(c p) -> p c", p=P)).then_inc(vectors_in, 16)
                act.dma_start(bias1[:, 0:D], proj_b.rearrange("(a d) -> a d", a=1).to_broadcast([P, D])).then_inc(vectors_in, 16)
                act.dma_start(a2_cols[:].rearrange("p w c -> p (w c)"), a2.rearrange("(w p) o -> p (w o)", p=P)).then_inc(vectors_in, 16)
                act.dma_start(a3_cols[:].rearrange("p w c -> p (w c)"), a3.rearrange("(w p) o -> p (w o)", p=P)).then_inc(vectors_in, 16)
                act.wait_ge(block_zero, 1)
                for side, vec in enumerate((a_fst, a_snd)):
                    for q in range(H):
                        c, row = divmod(q * C, P)
                        act.dma_start(a_block[row:row + C, c, side * H + q:side * H + q + 1],
                                      vec[q:q + 1, :].rearrange("a c -> c a")).then_inc(vectors_in, 16)
            act.wait_ge(setup_done, 1)

            def body(k, gru, att):
                kg = k - 1
                for what, arg in order:
                    if what == "init" and gru:
                        act.wait_ge(turn_filled, nth(k, TURN, arg))
                        act.activation(h_feat[arg][:].rearrange("p c t -> p (c t)"), turn_bank[:], ACT.Copy).then_inc(turn_drained, 1)
                    if what == "agg" and gru:
                        act.wait_ge(agg_filled, nth(k, 6, arg))
                        act.activation(u_hi[:].rearrange("p c t -> p (c t)"), agg_bank[:], ACT.Copy).then_inc(u_hi_ready, 1)
                    if what == "gates_u" and gru:
                        n, c = arg
                        act.wait_ge(gates_filled[c], nth(k, 6, n))
                        act.activation(tr[c][:], bank3(gates_rz[c], 2)[:, 0, :], ACT.Tanh,
                                       bias=half_b[:, c:c + 1], scale=0.5)
                        act.activation(hn[c][:], bank3(gates_ih[c], 2)[:, 1, :], ACT.Identity,
                                       bias=half_bh[:, 4 + c:5 + c], scale=0.5).then_inc(r_hn_ready[c], 1)
                        act.wait_ge(e_ready[c], k * 6 + n)
                        act.activation(tz[c][:], bank3(gates_rz[c], 2)[:, 1, :], ACT.Tanh,
                                       bias=half_b[:, KC + c:KC + c + 1], scale=0.5).then_inc(z_ready[c], 1)
                    if what == "gru" and gru:
                        n, c = arg
                        act.wait_ge(pre_ready[c], nth(k, 6, n))
                        act.activation(nn[c][:], pre[c][:], ACT.Tanh, bias=bi[:, 4 + c:5 + c]).then_inc(n_ready[c], 1)
                    if what == "turn" and gru and arg < SLOTS - NS:
                        act.wait_ge(turn_filled, nth(k, TURN, arg + 2))
                        act.activation(h_node[arg % 2][:].rearrange("p g d -> p (g d)"), turn_bank[:], ACT.Copy).then_inc(turn_drained, 1)
                    if what == "att" and att:
                        layer, kind, u = CONTENT[arg]
                        for s in range(NS):
                            bank = att_bank[s]
                            if kind == "T":
                                act.wait_ge(att_filled[s], nth(kg, NJ, arg))
                                act.activation(xT_hi[s][:].rearrange("p c t -> p (c t)"), bank[:], ACT.Copy).then_inc(xT_hi_ready[s], 1)
                            if kind == "P" and layer > 1:
                                act.wait_ge(att_filled[s], nth(kg, NJ, arg))
                                i = act.activation(h2[s][:, u, :], bank[:, 0:L2C], ACT.Copy)
                                i.then_inc(att_drained[s], 1)
                            if kind == "R":
                                act.wait_ge(att_filled[s], nth(kg, NJ, arg))
                                w = 48 if layer == 1 else 6
                                act.activation(rows[s][0:w].rearrange("r g i -> r (g i)"), bank[0:w, 0:P].bitcast(BF16),
                                               ACT.Copy).then_inc(att_drained[s], 1)
                            if kind == "X":
                                act.wait_ge(att_filled[s], nth(kg, NJ, arg))
                                w = 4 * P if layer == 1 else GS * P
                                e = prob[s][u % 2][:].rearrange("p a b -> p (a b)")[:, 0:w]
                                act.activation(e, bank[:, 0:w], ACT.Copy, scale=SLOPE).then_inc(scaled_ready[s], 1)
                            if kind == "Y" and u % 2 == 0:
                                act.wait_ge(att_filled[s], nth(kg, NJ, arg))
                                w = 4 if layer == 1 else GS
                                act.activation(probT[s][:, 0:w, :].rearrange("p a b -> p (a b)"), bank[:, 0:w * P],
                                               ACT.Copy).then_inc(att_drained[s], 1)
                    if what == "att2" and att:
                        layer, kind, u = CONTENT[arg]
                        for s in range(NS):
                            if kind == "X" and layer == 1:
                                act.wait_ge(shifted[s], nth(kg, 4, u))
                                e = prob[s][u % 2][:]
                                act.activation(e, e, ACT.Exp).then_inc(prob_ready[s], 1)
                            if kind == "X" and layer > 1:
                                act.wait_ge(mtop_ready[s], nth(kg, 6, 2 + layer))
                                act.wait_ge(att_drained[s], nth(kg, NJ, arg))
                                for g in range(GS):
                                    last = act.activation(prob[s][0][:, g, :], prob[s][0][:, g, :], ACT.Exp,
                                                       bias=mtop[s][0][:, g:g + 1], accum_out=zsum[s][:, g:g + 1])
                                last.then_inc(summed[s], 1)
                            if kind == "A" and layer == 2:
                                act.wait_ge(below_ready[s], nth(kg, 1, 0))
                                act.activation(below[s][:], below[s][:], ACT.Exp).then_inc(elu_ready[s], 1)

            body(0, True, False)
            with act.Fori(1, NB) as k:
                body(k, True, True)
            body(NB, False, True)

        @block.vector
        def _(dve):
            dve.memset(a_block[:], 0.0).then_inc(block_zero, 1)
            for s in range(NS):
                last = dve.memset(h1[s][:], 1.0)
            last.then_inc(setup_dve, 1)
            dve.wait_ge(ident_ready, 1)
            dve.tensor_copy(ident_b[:], ident[:]).then_inc(setup_dve, 1)
            dve.tensor_tensor(pick16[:], ident[0:48, 0:16], ident[0:48, 16:32], ALU.add)
            dve.tensor_tensor(pick2[:], ident[0:6, 0:2], ident[0:6, 2:4], ALU.add).then_inc(setup_dve, 1)
            dve.wait_ge(setup_dve, 3)
            dve.tensor_tensor(pick16[:], pick16[:], ident[0:48, 32:48], ALU.add)
            dve.tensor_tensor(pick2[:], pick2[:], ident[0:6, 4:6], ALU.add).then_inc(setup_dve, 1)
            dve.wait_ge(setup_dve, 4)
            dve.tensor_copy(sel16[:], pick16[:].unsqueeze(2).to_broadcast([48, 16, P]))
            dve.tensor_copy(sel2[:], pick2[:].unsqueeze(2).to_broadcast([6, 2, P]))
            dve.wait_ge(vectors_in, 16 * N_VECTORS)
            dve.tensor_copy(b_wide[:], b_col[:].unsqueeze(2).to_broadcast([P, KC, P])).then_inc(setup_dve, 1)
            dve.tensor_tensor(bsum[:], bi[:], bh[:], ALU.add).then_inc(setup_dve, 1)
            dve.tensor_scalar(half_bh[:], bh[:], 0.5, None, ALU.mult)
            dve.wait_ge(setup_dve, 6)

            def two_parts(hi, lo, src, n):
                dve.tensor_copy(hi, src).then_inc(setup_hi, 1)
                dve.wait_ge(setup_hi, n)
                return dve.tensor_tensor(lo, src, hi.bitcast(F32), ALU.subtract)

            dve.wait_ge(weights_in, 16 * N_WEIGHTS)
            two_parts(p1_hi[:, :, 0:D], p1_lo[:, :, 0:D], raw_p1[:], 1)
            two_parts(p2_hi[:, :, 0:D], p2_lo[:, :, 0:D], raw_p2[:], 2)
            pairs = 2
            for q, (what, m, i) in enumerate(panels):
                bank = setup_bank[q % 2]
                dve.wait_ge(setup_filled, q + 1)
                if what == "turn" and m in ("ih", "w", "p1", "p2"):
                    to = {"ih": wihT, "w": wT, "p1": p1T, "p2": p2T}[m]
                    if m == "ih":
                        to = to[:].rearrange("p k e -> p (k e)")[:, i * 512:(i + 1) * 512]
                    elif m == "w":
                        to = to[:, i].rearrange("p k e -> p (k e)")
                    else:
                        to = to[:].rearrange("p k e -> p (k e)")
                    dve.tensor_copy(to, bank[:]).then_inc(setup_drained, 1)
                    continue
                if what == "turn" and m == "hh":
                    hi, lo = (t[:].rearrange("p k e -> p (k e)")[:, i * 512:(i + 1) * 512] for t in (whh_hi, whh_lo))
                    src = bank[:]
                elif what == "turn":
                    hi, lo, src = p3_hi[:, :, 0:D], p3_lo[:, :, 0:D], bank3(bank, KC)
                elif what == "fold":
                    dc, nh = i
                    n0, n1 = ((0, 512), (512, G3))[nh]
                    hi, lo, src = wc_hi[:, m, dc, n0:n1], wc_lo[:, m, dc, n0:n1], bank[:, 0:n1 - n0]
                elif m == "bias":
                    dve.tensor_copy(bias1[:, D:L1C], bank[:, 0:2 * H]).then_inc(setup_drained, 1)
                    continue
                else:
                    hi, lo, w = {"p1": (p1_hi, p1_lo, L1C), "p2": (p2_hi, p2_lo, L2C), "p3": (p3_hi, p3_lo, L2C)}[m]
                    hi, lo, src = hi[:, i, D:w], lo[:, i, D:w], bank[:, 0:w - D]
                pairs += 1
                two_parts(hi, lo, src, pairs).then_inc(setup_drained, 1)
            dve.wait_ge(setup_drained, len(panels))
            dve.tensor_scalar(half_b[:], bsum[:], 0.5, None, ALU.mult).then_inc(setup_done, 1)

            def norm_stats(s, kg, i, src):
                if i == 0:
                    dve.wait_ge(turn_drained, nth(kg, TURN, SLOTS + s))
                elif i == 3:
                    dve.wait_ge(att_drained[s], nth(kg, NJ, NJ - 1))
                else:
                    dve.wait_ge(y_ready[s], nth(kg, 2, i - 1))
                for g in range(GS):
                    last = dve.bn_stats(stats[s][:, g, :], src[:, g, :])
                last.then_inc(stats_ready[s], 1)
                dve.wait_ge(stats_ready[s], nth(kg, 4, i))
                dve.nop(nofuse=True)
                for g in range(GS):
                    last = dve.bn_aggr(mv[s][:, g, :], stats[s][:, g, :])
                last.then_inc(mv_ready[s], 1)
                dve.wait_ge(mv_ready[s], nth(kg, 4, i))
                dve.tensor_scalar(veps[s][:], mv[s][:, :, 1], EPS, None, ALU.add).then_inc(veps_ready[s], 1)

            def norm_apply(s, kg, i, src):
                dve.wait_ge(rstd_ready[s], nth(kg, 4, i))
                if i == 3:
                    dve.wait_ge(stored[s], 16 * kg + 1)
                to = result[s] if i == 3 else xn[s]
                for g in range(GS):
                    last = dve.tensor_scalar(to[:, g, :], src[:, g, :], mv[s][:, g, 0:1], rstd[s][:, g:g + 1],
                                             ALU.subtract, ALU.mult)
                last.then_inc(result_ready[s] if i == 3 else xn_ready[s], 1)

            def body(k, gru, att):
                kg = k - 1
                for what, arg in order:
                    if what == "begin" and gru:
                        for s in range(NS):
                            dve.wait_ge(adj_loaded[s], 16 * (k + 1))
                            dve.wait_ge(neg_moved[s], k * 2)
                            dve.tensor_scalar(edges[s][:], adj_in[s][:], 0, None, ALU.not_equal).then_inc(masks_ready[s], 1)
                            dve.tensor_scalar(neg1_next[s][:], adj_in[s][:], 1, MASKED, ALU.not_equal, ALU.mult).then_inc(masks_ready[s], 1)
                            dve.tensor_scalar(neg3_next[s][:], adj_in[s][:], 0, MASKED, ALU.is_le, ALU.mult).then_inc(masks_ready[s], 1)
                    if what == "begin" and att:
                        for s in range(NS):
                            norm_stats(s, kg, 0, y0[s])
                        for s in range(NS):
                            norm_apply(s, kg, 0, y0[s])
                    if what == "agg" and gru:
                        dve.wait_ge(u_hi_ready, nth(k, 6, arg))
                        dve.tensor_tensor(u_lo[:].rearrange("p c t -> p (c t)"), agg_bank[:],
                                          u_hi[:].rearrange("p c t -> p (c t)").bitcast(F32), ALU.subtract).then_inc(u_ready, 1)
                    if what == "gates_u" and gru:
                        n, c = arg
                        dve.wait_ge(r_hn_ready[c], nth(k, 6, n))
                        dve.scalar_tensor_tensor(pre[c][:], tr[c][:], 1.0, hn[c][:], ALU.add, ALU.mult).then_inc(q_ready[c], 1)
                        dve.wait_ge(q_ready[c], nth(k, 6, n))
                        dve.tensor_tensor(pre[c][:], bank3(gates_ih[c], 2)[:, 0, :], pre[c][:], ALU.add).then_inc(pre_ready[c], 1)
                    if what == "gru" and gru:
                        n, c = arg
                        s = n % 2
                        dve.wait_ge(d_ready[c], nth(k, 6, n))
                        dve.wait_ge(z_ready[c], nth(k, 6, n))
                        dve.scalar_tensor_tensor(dd[c][:], tz[c][:], 1.0, dd[c][:], ALU.add, ALU.mult).then_inc(e_ready[c], 1)
                        dve.wait_ge(e_ready[c], nth(k, 6, n))
                        dve.scalar_tensor_tensor(h_feat[s][:, c, :], dd[c][:], 0.5, nn[c][:], ALU.mult, ALU.add).then_inc(h_ready[c], 1)
                    if what == "turn" and gru and arg >= SLOTS - NS:
                        s = arg % 2
                        dve.wait_ge(turn_filled, nth(k, TURN, arg + 2))
                        dve.tensor_tensor(y0[s][:].rearrange("p g d -> p (g d)"), turn_bank[:],
                                          x_keep[s][:].rearrange("p g d -> p (g d)"), ALU.add).then_inc(turn_drained, 1)
                    if what == "att" and att:
                        layer, kind, u = CONTENT[arg]
                        for s in range(NS):
                            attend(s, kg, arg, layer, kind, u)
                    if what == "att2" and att:
                        layer, kind, u = CONTENT[arg]
                        for s in range(NS):
                            attend2(s, kg, arg, layer, kind, u)
                    if what == "att3" and att and CONTENT[arg] == (2, "A", 0):
                        for s in range(NS):
                            norm_apply(s, kg, 2, y[s])

            def attend(s, kg, j, layer, kind, u):
                bank = att_bank[s]
                filled = nth(kg, NJ, j)
                if kind == "T":
                    dve.wait_ge(xT_hi_ready[s], nth(kg, 3, layer - 1))
                    dve.tensor_tensor(xT_lo[s][:].rearrange("p c t -> p (c t)"), bank[:],
                                      xT_hi[s][:].rearrange("p c t -> p (c t)").bitcast(F32), ALU.subtract).then_inc(att_drained[s], 1)
                if kind == "P" and layer == 1:
                    dve.wait_ge(att_filled[s], filled)
                    dve.tensor_tensor(h1[s][:, u, :, 0:C], bank[:, 0:D].rearrange("p (h c) -> p h c", h=H),
                                      bias1[:, 0:D].rearrange("p (h c) -> p h c", h=H), ALU.add)
                    last = dve.tensor_tensor(terms[s][:, u, :], bank[:, D:L1C], bias1[:, D:L1C], ALU.add)
                    last.then_inc(att_drained[s], 1)
                if kind == "X":
                    n, w = (4, 4) if layer == 1 else (GS, GS)
                    i = u if layer == 1 else 2 + layer
                    tp, mt = top[s][u % 2][:, 0:n], mtop[s][u % 2][:, 0:n]
                    e = prob[s][u % 2][:, 0:w, :]
                    b = bank[:, 0:w * P].rearrange("p (a b) -> p a b", a=w)
                    dve.wait_ge(scaled_ready[s], nth(kg, 6, i))
                    dve.tensor_reduce(tp, b, AX.X, ALU.max).then_inc(top_ready[s], 1)
                    dve.tensor_tensor(e, b, e, ALU.max).then_inc(att_drained[s], 1)
                    dve.wait_ge(top_ready[s], nth(kg, 6, i))
                    if layer == 1:
                        dve.scalar_tensor_tensor(mt, tp, SLOPE, tp, ALU.mult, ALU.max).then_inc(mtop_ready[s], 1)
                    else:
                        dve.tensor_scalar(rz[s][:, 0:n], tp, -1.0, None, ALU.mult).then_inc(rz_ready[s], 1)
                        dve.wait_ge(rz_ready[s], nth(kg, 6, (2, 4)[layer - 2]))
                        dve.scalar_tensor_tensor(mt, tp, -SLOPE, rz[s][:, 0:n], ALU.mult, ALU.min).then_inc(mtop_ready[s], 1)
                if kind == "Y" and u % 2 == 1:
                    dve.wait_ge(att_filled[s], filled)
                    dve.tensor_copy(probT[s][:, 4:8, :].rearrange("p a b -> p (a b)"), bank[:]).then_inc(att_drained[s], 1)
                if kind == "A" and layer == 1:
                    dve.wait_ge(att_filled[s], filled)
                    o = bank[:, 0:H * (C + 1)].rearrange("p (h c) -> p h c", h=H)
                    dve.reciprocal(rz[s][:], o[:, :, C]).then_inc(rz_ready[s], 1)
                    dve.wait_ge(rz_ready[s], nth(kg, 6, u))
                    dve.tensor_tensor(y[s][:, u].rearrange("p (h c) -> p h c", h=H), o[:, :, 0:C],
                                      rz[s][:].unsqueeze(2).to_broadcast([P, H, C]), ALU.mult).then_inc(att_drained[s], 1)
                    if u == 1:
                        dve.wait_ge(att_drained[s], filled)
                        dve.tensor_tensor(y[s][:], y[s][:], xn[s][:], ALU.add).then_inc(y_ready[s], 1)
                        norm_stats(s, kg, 1, y[s])
                if kind == "A" and layer == 2:
                    dve.wait_ge(att_filled[s], filled)
                    dve.tensor_scalar(below[s][:].rearrange("p g d -> p (g d)"), bank[:], 0.0, None, ALU.min).then_inc(below_ready[s], 1)
                if kind == "A" and layer == 3:
                    dve.wait_ge(att_filled[s], filled)
                    dve.wait_ge(rz_ready[s], nth(kg, 6, 5))
                    for g in range(GS):
                        last = dve.scalar_tensor_tensor(y[s][:, g, :], bank[:, g * D:(g + 1) * D], rz[s][:, g:g + 1],
                                                        xn[s][:, g, :], ALU.mult, ALU.add)
                    last.then_inc(att_drained[s], 1)
                    norm_stats(s, kg, 3, y[s])

            def attend2(s, kg, j, layer, kind, u):
                bank = att_bank[s]
                if kind == "X" and layer > 1:
                    dve.wait_ge(summed[s], nth(kg, 2, layer - 2))
                    dve.reciprocal(rz[s][:, 0:GS], zsum[s][:]).then_inc(rz_ready[s], 1)
                    if layer == 2:
                        dve.wait_ge(rz_ready[s], nth(kg, 6, 3))
                        for g in range(GS):
                            last = dve.tensor_scalar(prob[s][0][:, g, :], prob[s][0][:, g, :], rz[s][:, g:g + 1], None, ALU.mult)
                        last.then_inc(prob_ready[s], 1)
                if kind == "A" and layer == 1 and u == 1:
                    norm_apply(s, kg, 1, y[s])
                if kind == "A" and layer == 2:
                    dve.wait_ge(elu_ready[s], nth(kg, 1, 0))
                    b = below[s][:].rearrange("p g d -> p (g d)")
                    dve.scalar_tensor_tensor(b, bank[:], 0.0, b, ALU.max, ALU.add).then_inc(att_drained[s], 1)
                    dve.wait_ge(att_drained[s], nth(kg, NJ, j))
                    dve.scalar_tensor_tensor(y[s][:], below[s][:], -1.0, xn[s][:], ALU.add, ALU.add).then_inc(y_ready[s], 1)
                    norm_stats(s, kg, 2, y[s])
                if kind == "A" and layer == 3:
                    norm_apply(s, kg, 3, y[s])

            body(0, True, False)
            with dve.Fori(1, NB) as k:
                body(k, True, True)
            body(NB, False, True)


_INS = ["x", "adj", "L0_gnn_weight", "L0_gnn_w_ih", "L0_gnn_w_hh", "L0_gnn_b_ih", "L0_gnn_b_hh", "L1_gnn_proj_kernel",
        "L1_gnn_proj_bias", "L1_gnn_attn_fst", "L1_gnn_attn_snd", "L2_gnn_W", "L2_gnn_a", "L3_gnn_W", "L3_gnn_a"]


def kernel(**inputs):
    import numpy as _np
    import concourse.bacc as _bacc
    from concourse import mybir as _mybir
    from concourse.bass_utils import run_bass_kernel_spmd as _run

    nc = _bacc.Bacc("TRN2", target_bir_lowering=False, num_devices=1)
    arrays, args = {}, []
    for name in _INS:
        a = _np.ascontiguousarray(inputs[name])
        arrays[f"in_{name}"] = a
        args.append(nc.dram_tensor(f"in_{name}", a.shape, _mybir.dt.from_np(a.dtype), kind="ExternalInput").ap())
    shape = arrays["in_x"].shape
    args.append(nc.dram_tensor("out_0", shape, _mybir.dt.float32, kind="ExternalOutput").ap())
    graph_layers(nc, *args)
    r = _run(nc, [arrays], core_ids=[0])
    return r.results[0]["out_0"]
```

```python
from contextlib import ExitStack

import concourse.bass as bass
from concourse import mybir

ALU = mybir.AluOpType
ACT = mybir.ActivationFunctionType
AX = mybir.AxisListType
F32 = mybir.dt.float32
F32R = mybir.dt.float32r
BF16 = mybir.dt.bfloat16
I32 = mybir.dt.int32

P = 128
GS = 2
NS = 2
TOK = GS * P
MASKED = -9.0e15
SLOPE = 0.2
EPS = 1e-5
SLOTS = 6

LATE = {("gru", (SLOTS - 1, 1)), ("turn", SLOTS - 1)}
EARLY = {("keep", 0), ("edges", 0), ("init", 0)}

CONTENT = [(1, "T", 0), (1, "P", 0), (1, "P", 1), (1, "R", 0), (1, "X", 0), (1, "X", 1), (1, "Y", 0),
           (1, "X", 2), (1, "Y", 1), (1, "A", 0), (1, "X", 3), (1, "Y", 2), (1, "Y", 3), (1, "A", 1),
           (2, "T", 0), (2, "P", 0), (2, "P", 1), (2, "R", 0), (2, "X", 0), (2, "A", 0),
           (3, "T", 0), (3, "P", 0), (3, "P", 1), (3, "R", 0), (3, "X", 0), (3, "Y", 0), (3, "A", 0)]
NJ = len(CONTENT)
POS = {c: j for j, c in enumerate(CONTENT)}


TIMES = {(1, "T"): (850, 2600, ()), (1, "P"): (700, 1400, ()), (1, "R"): (150, 900, ()),
         (1, "X"): (700, 2900, (2500, 3800)), (1, "Y"): (850, 1700, ()), (1, "A"): (850, 1900, ()),
         (2, "T"): (850, 2600, ()), (2, "P"): (700, 1400, ()), (2, "R"): (150, 900, ()),
         (2, "X"): (350, 4300, (1900, 2900)), (2, "A"): (900, 7500, (1900, 2800, 5500)),
         (3, "T"): (850, 2600, ()), (3, "P"): (700, 1400, ()), (3, "R"): (150, 900, ()),
         (3, "X"): (350, 3400, (1900, 2900)), (3, "Y"): (450, 1300, ()), (3, "A"): (900, 4500, (4000,))}
SPECIAL = {(1, "P", 1): (700, 4200, ()), (2, "P", 1): (700, 4200, ()), (3, "P", 1): (700, 4200, ()),
           (1, "A", 1): (850, 6000, (4500,))}
STRETCH = 1.25


def make_schedule():
    def gates(kind, n, c):
        return [((kind, (n, c, gate)), 654) for gate in range(3)]

    core = [(("edges", 1), 0), (("norm0", 0), 0), (("agg", 0), 853), (("norm0b", 0), 0), (("negs", 0), 0)]
    core += gates("gates_h", 0, 0) + gates("gates_u", 0, 0)
    core += [(("turn", SLOTS - 1), 853), (("keep", 1), 0), (("norm0", 1), 0), (("negs", 1), 0)]
    core += gates("gates_h", 0, 1)
    core += [(("norm0b", 1), 0), (("init", 1), 853)] + gates("gates_u", 0, 1)
    for n in range(1, SLOTS):
        core += [(("agg", n), 853)] + gates("gates_h", n, 0) + gates("gates_u", n, 0) + [(("turn", n - 1), 853)]
        last = n == SLOTS - 1
        core += [(("keep", 0), 0), (("edges", 0), 0)] if last else []
        core += gates("gates_h", n, 1)
        after = gates("gates_u", n, 1)
        core += after[:1] + ([(("init", 0), 853)] if last else []) + after[1:]

    order, t = [], 0
    waiting = [(0, ("gru", (SLOTS - 1, 1)))]
    turn = [[1 << 50, 0] for _ in range(NS)]

    def due(now):
        waiting.sort(key=lambda w: w[0])
        while waiting and waiting[0][0] <= now:
            order.append(waiting.pop(0)[1])

    def contents(now, limit):
        t = now
        for s in range(NS):
            start, j = turn[s]
            if j < NJ and start <= limit:
                due(t)
                spent, lag, phases = SPECIAL.get(CONTENT[j]) or TIMES[CONTENT[j][:2]]
                for w in [w for w in waiting if w[1][0] == "att" and w[1][1][0] == s and needs(j, w[1][1][1])]:
                    waiting.remove(w)
                    order.append(w[1])
                order.append(("att", (s, j, 0)))
                waiting.extend((t + p, ("att", (s, j, i + 1))) for i, p in enumerate(phases))
                t += spent
                turn[s] = [t + (lag - spent) * STRETCH, j + 1]
                if CONTENT[j] == (3, "X", 0):
                    waiting.append((t + 2000, ("end", s)))
        return t

    for item, spent in core:
        t = contents(t, t)
        due(t)
        order.append(item)
        t += spent
        if item[0] == "norm0b":
            turn[item[1]][0] = t + 800
        if item[0] == "gates_h" and item[1][1:] == (1, 2):
            waiting.append((t, ("gru", (item[1][0], 0))))
        if item[0] == "gates_u" and item[1][1:] == (1, 2) and item[1][0] < SLOTS - 1:
            waiting.append((t + 1200, ("gru", (item[1][0], 1))))
    while any(j < NJ for _, j in turn):
        t = contents(max(t, min(start for start, j in turn if j < NJ)), 1 << 40)
    due(1 << 40)
    return order


def needs(j, i):
    layer, kind, u = CONTENT[j]
    return CONTENT[i][0] < layer or (kind in "YA" and CONTENT[i][1] == "X" and (layer > 1 or (kind == "Y" and CONTENT[i][2] <= u)))


def graph_layers(nc, x, adj, weight, w_ih, w_hh, b_ih, b_hh, proj, proj_b, a_fst, a_snd, W2, a2, W3, a3, out):
    B, N, D = x.shape
    L = weight.shape[0]
    H, C = a_fst.shape
    G3 = 3 * D
    KC = D // P
    NB = B // (GS * NS)
    L1C, L2C = D + 2 * H, D + 2
    assert (N, D, L, H * C) == (P, 256, 3, D)
    order = make_schedule()

    with ExitStack() as ctx:
        def sb(name, shape, dt=F32):
            return ctx.enter_context(nc.sbuf_tensor(name, shape, dt))

        def psum(name):
            return ctx.enter_context(nc.psum_tensor(name, [P, 512], F32))

        def sem(name):
            return ctx.enter_context(nc.semaphore(name))

        def sems(name, n=NS):
            return [sem(f"{name}_{i}") for i in range(n)]

        gates_rz = [psum(f"gates_rz_{c}") for c in range(KC)]
        gates_ih = [psum(f"gates_ih_{c}") for c in range(KC)]
        agg_bank = psum("agg_bank")
        turn_bank = psum("turn_bank")
        att_bank = [psum(f"att_bank_{s}") for s in range(NS)]

        whh_hi, whh_lo = (sb(n, [P, KC, G3], F32R) for n in ("whh_hi", "whh_lo"))
        wc_hi, wc_lo = (sb(n, [P, L, KC, G3], F32R) for n in ("wc_hi", "wc_lo"))
        p1_hi, p1_lo = (sb(n, [P, KC, L1C], F32R) for n in ("p1_hi", "p1_lo"))
        p2_hi, p2_lo = (sb(n, [P, KC, L2C], F32R) for n in ("p2_hi", "p2_lo"))
        p3_hi, p3_lo = (sb(n, [P, KC, L2C], F32R) for n in ("p3_hi", "p3_lo"))
        bias1 = sb("bias1", [P, L1C])
        bi, bh, bsum, half_b, half_bh = (sb(n, [P, 6]) for n in ("bi", "bh", "bsum", "half_b", "half_bh"))
        ident = sb("ident", [P, P])
        ident_b = sb("ident_b", [P, P], BF16)
        pick16 = sb("pick16", [48, 16])
        pick2 = sb("pick2", [6, 2])
        sel16 = sb("sel16", [48, 16, P], BF16)
        sel2 = sb("sel2", [6, 2, P], BF16)
        minus_half = sb("minus_half", [P, GS])

        x_in = [sb(f"x_in_{s}", [P, GS, D]) for s in range(NS)]
        adj_in = [sb(f"adj_in_{s}", [P, GS, P], I32) for s in range(NS)]
        x_keep = [sb(f"x_keep_{s}", [P, GS, D]) for s in range(NS)]
        edges = [sb(f"edges_{s}", [P, GS, P]) for s in range(NS)]
        neg1_next = [sb(f"neg1_next_{s}", [P, GS, P], BF16) for s in range(NS)]
        neg3_next = [sb(f"neg3_next_{s}", [P, GS, P], BF16) for s in range(NS)]
        h_feat = [sb(f"h_feat_{s}", [P, KC, TOK]) for s in range(NS)]
        h_hi = [sb(f"h_hi_{s}", [P, KC, TOK], F32R) for s in range(NS)]
        h_lo = [sb(f"h_lo_{s}", [P, KC, TOK], F32R) for s in range(NS)]
        h_node = [sb(f"h_node_{s}", [P, GS, D]) for s in range(NS)]
        u_hi, u_lo = (sb(n, [P, KC, TOK], F32R) for n in ("u_hi", "u_lo"))
        tr, tz, hn, pre, nn, dd = ([sb(f"{n}_{c}", [P, TOK]) for c in range(KC)]
                                   for n in ("tr", "tz", "hn", "pre", "nn", "dd"))
        y = [sb(f"y_{s}", [P, GS, D]) for s in range(NS)]
        y0 = [sb(f"y0_{s}", [P, GS, D]) for s in range(NS)]
        xn = [sb(f"xn_{s}", [P, GS, D]) for s in range(NS)]
        xT_hi = [sb(f"xT_hi_{s}", [P, KC, TOK], F32R) for s in range(NS)]
        xT_lo = [sb(f"xT_lo_{s}", [P, KC, TOK], F32R) for s in range(NS)]
        neg1 = [sb(f"neg1_{s}", [P, GS, P], BF16) for s in range(NS)]
        neg3 = [sb(f"neg3_{s}", [P, GS, P], BF16) for s in range(NS)]
        h1 = [sb(f"h1_{s}", [P, GS, H, C + 1]) for s in range(NS)]
        h2 = [sb(f"h2_{s}", [P, GS, L2C]) for s in range(NS)]
        terms = [sb(f"terms_{s}", [P, GS, 2 * H]) for s in range(NS)]
        rest = [sb(f"rest_{s}", [P, GS, 2 * H]) for s in range(NS)]
        parts = [sb(f"parts_{s}", [P, GS, 3, 2 * H], BF16) for s in range(NS)]
        parts2 = [sb(f"parts2_{s}", [P, GS, 3, 2], BF16) for s in range(NS)]
        rows = [sb(f"rows_{s}", [48, GS, P], BF16) for s in range(NS)]
        prob = [[sb(f"prob_{s}_{i}", [P, 4, P]) for i in range(2)] for s in range(NS)]
        top = [[sb(f"top_{s}_{i}", [P, 4]) for i in range(2)] for s in range(NS)]
        mtop = [[sb(f"mtop_{s}_{i}", [P, 4]) for i in range(2)] for s in range(NS)]
        probT = [sb(f"probT_{s}", [P, H, P]) for s in range(NS)]
        zsum = [sb(f"zsum_{s}", [P, GS]) for s in range(NS)]
        rz = [sb(f"rz_{s}", [P, H]) for s in range(NS)]
        below = [sb(f"below_{s}", [P, GS, D]) for s in range(NS)]
        stats = [sb(f"stats_{s}", [P, GS, 6]) for s in range(NS)]
        mv = [sb(f"mv_{s}", [P, GS, 2]) for s in range(NS)]
        veps = [sb(f"veps_{s}", [P, GS]) for s in range(NS)]
        rstd = [sb(f"rstd_{s}", [P, GS]) for s in range(NS)]
        result = [sb(f"result_{s}", [P, GS, D]) for s in range(NS)]
        raw_ih, raw_hh = (sb(n, [P, 6, D]) for n in ("raw_ih", "raw_hh"))
        raw_w = sb("raw_w", [P, L, KC, D])
        raw_p1, raw_p2, raw_p3, p1T, p2T = result[0], result[1], y[0], below[0], below[1]
        wihT = sb("wihT", [P, KC, G3])
        wT = sb("wT", [P, L, KC, D])
        a_block = sb("a_block", [P, KC, 2 * H])
        a2_cols, a3_cols = (sb(n, [P, 2, KC]) for n in ("a2_cols", "a3_cols"))
        b_col = sb("b_col", [P, KC])
        b_wide = sb("b_wide", [P, KC, P])

        ident_zero, ident_ready, block_zero, half_ready = (sem(n) for n in ("ident_zero", "ident_ready", "block_zero", "half_ready"))
        weights_in, vectors_in = sem("weights_in"), sem("vectors_in")
        setup_filled, setup_drained, setup_dve, setup_hi, setup_done = (
            sem(n) for n in ("setup_filled", "setup_drained", "setup_dve", "setup_hi", "setup_done"))
        x_loaded, adj_loaded, x_kept, edges_ready, negs_ready = (sems(n) for n in ("x_loaded", "adj_loaded", "x_kept", "edges_ready", "negs_ready"))
        gates_filled, h_used, r_hn_ready, z_ready, q_ready, pre_ready, n_ready, d_ready, e_ready, h_ready = (
            sems(n, KC) for n in ("gates_filled", "h_used", "r_hn_ready", "z_ready", "q_ready", "pre_ready",
                                  "n_ready", "d_ready", "e_ready", "h_ready"))
        h_hi_ready, h_lo_ready = sems("h_hi_ready"), sems("h_lo_ready")
        agg_filled, u_hi_ready, u_ready = sem("agg_filled"), sem("u_hi_ready"), sem("u_ready")
        turn_filled, turn_drained = sem("turn_filled"), sem("turn_drained")
        neg_moved = sems("neg_moved")
        att_filled, att_drained, xT_hi_ready, cut_done, rest_done, parts_ready = (
            sems(n) for n in ("att_filled", "att_drained", "xT_hi_ready", "cut_done", "rest_done", "parts_ready"))
        scaled_ready, top_ready, mtop_ready, shifted, summed, prob_ready, rz_ready = (
            sems(n) for n in ("scaled_ready", "top_ready", "mtop_ready", "shifted", "summed", "prob_ready", "rz_ready"))
        below_ready, elu_ready, y_ready, stats_ready, mv_ready, veps_ready, rstd_ready, xn_ready, result_ready, stored = (
            sems(n) for n in ("below_ready", "elu_ready", "y_ready", "stats_ready", "mv_ready", "veps_ready", "rstd_ready",
                              "xn_ready", "result_ready", "stored"))

        def nth(k, per, i):
            return k * per + (i + 1)

        x_v = x.rearrange("(k s g) n d -> k s n g d", s=NS, g=GS)
        adj_v = adj.rearrange("(k s g) n m -> k s n g m", s=NS, g=GS)
        out_v = out.rearrange("(k s g) n d -> k s n g d", s=NS, g=GS)

        TURN = 8

        def part_of(part, k, gru, att, more):
            kind, late = part[0], part in LATE
            if late or kind in ("att", "norm0", "norm0b"):
                return *part, k - 1, att
            if part in EARLY:
                return *part, k + 1, gru and more
            return *part, k, gru

        def turn5(kk):
            return nth(kk + 1, TURN, 0) - (isinstance(kk, int) and kk == NB - 1)

        def init_turn(s, k):
            return nth(k, TURN, 1) if s else (1 if isinstance(k, int) and k == 0 else k * TURN)

        def y0_count(s, k):
            return turn5(k) if s else nth(k, TURN, SLOTS)

        def flat(tile):
            return tile[:].rearrange("p a b -> p (a b)")

        def bank3(bank, a):
            return bank[:].rearrange("p (a b) -> p a b", a=a)

        panels = [("turn", "ih", i) for i in range(3)] + [("turn", "w", i) for i in range(L)]
        panels += [("turn", "hh", i) for i in range(3)] + [("turn", m, 0) for m in ("p1", "p2", "p3")]
        panels += [("fold", i, (dc, nh)) for i in range(L) for dc in range(KC) for nh in range(2)]
        panels += [("terms", m, dc) for m in ("p1", "p2", "p3") for dc in range(KC)] + [("terms", "bias", 0)]
        setup_bank = [agg_bank, turn_bank]
        N_WEIGHTS, N_VECTORS = 6, 6 + 2 * H

        block = ctx.enter_context(nc.Block())

        @block.sync
        def _(sp):
            def load(k):
                for s in range(NS):
                    if not (isinstance(k, int) and k == 0):
                        sp.wait_ge(x_kept[s], k)
                        sp.nop(nofuse=True)
                        sp.wait_ge(edges_ready[s], k)
                        sp.nop(nofuse=True)
                        sp.wait_ge(negs_ready[s], k * 2)
                        sp.nop(nofuse=True)
                    sp.dma_start(x_in[s][:], x_v[k, s]).then_inc(x_loaded[s], 16)
                    sp.dma_start(adj_in[s][:], adj_v[k, s]).then_inc(adj_loaded[s], 16)

            def store(kg):
                for s in range(NS):
                    sp.wait_ge(result_ready[s], nth(kg, 1, 0))
                    sp.nop(nofuse=True)
                    sp.dma_start(out_v[kg, s], result[s][:]).then_inc(stored[s], 16)

            sp.dma_start(raw_ih[:], w_ih.rearrange("(c p) d -> p c d", p=P)).then_inc(weights_in, 16)
            sp.dma_start(raw_w[:], weight.rearrange("l (c p) d -> p l c d", p=P)).then_inc(weights_in, 16)
            sp.dma_start(raw_hh[:], w_hh.rearrange("(c p) d -> p c d", p=P)).then_inc(weights_in, 16)
            for raw, src in ((raw_p1, proj), (raw_p2, W2), (raw_p3, W3)):
                sp.dma_start(raw[:], src.rearrange("(c p) d -> p c d", p=P)).then_inc(weights_in, 16)
            load(0)
            load(1)
            with sp.Fori(1, NB - 1) as k:
                load(k + 1)
                store(k - 1)
            store(NB - 2)
            store(NB - 1)
            for s in range(NS):
                sp.wait_ge(stored[s], 16 * NB + 1)

        @block.gpsimd
        def _(pool):
            pool.memset(ident[:], 0.0).then_inc(ident_zero, 1)
            pool.wait_ge(ident_zero, 1)
            pool.affine_select(out=ident[:], in_=ident[:], compare_op=ALU.not_equal, fill=1.0, base=0,
                               pattern=[[-1, P]], channel_multiplier=1).then_inc(ident_ready, 1)
            pool.memset(minus_half[:], -0.5).then_inc(half_ready, 1)
            pool.wait_ge(half_ready, 1)
            for s in range(NS):
                pool.memset(rstd[s][:], 1.0).then_inc(stored[s], 1)

            def body(k, gru, att, more=True):
                for part in order:
                    what, arg, kk, on = part_of(part, k, gru, att, more)
                    if not on:
                        continue
                    if what == "keep":
                        keep(arg, kk)
                    if what == "init":
                        init(arg, kk)
                    if what == "norm0":
                        inv_std(arg, kk, 0)
                    if what == "gru":
                        n, c = arg
                        s = n % 2
                        pool.wait_ge(n_ready[c], nth(kk, 6, n))
                        pool.tensor_tensor(dd[c][:], h_feat[s][:, c, :], nn[c][:], ALU.subtract).then_inc(d_ready[c], 1)
                        if n < SLOTS - NS:
                            i = 1 + 2 * (n // 2) + c
                            pool.wait_ge(h_used[1], nth(kk, 6, n))
                            pool.wait_ge(h_ready[c], nth(kk, 6, n))
                            pool.nop(nofuse=True)
                            pool.tensor_copy(h_hi[s][:, c, :], h_feat[s][:, c, :]).then_inc(h_hi_ready[s], 1)
                            pool.wait_ge(h_hi_ready[s], nth(kk, 5, i))
                            pool.tensor_tensor(h_lo[s][:, c, :], h_feat[s][:, c, :], h_hi[s][:, c, :].bitcast(F32),
                                               ALU.subtract).then_inc(h_lo_ready[s], 1)
                    if what == "att":
                        s, j, phase = arg
                        layer, kind, u = CONTENT[j]
                        if (kind, u, phase) == ("P", GS - 1, 0):
                            cut_terms(s, kk, layer)
                        if kind == "X" and layer == 1 and phase == 1:
                            pool.wait_ge(mtop_ready[s], nth(kk, 6, u))
                            pool.wait_ge(att_drained[s], nth(kk, NJ, j))
                            e = prob[s][u % 2][:]
                            m = mtop[s][u % 2][:, 0:4].unsqueeze(2).to_broadcast([P, 4, P])
                            pool.tensor_tensor(e, e, m, ALU.subtract).then_inc(shifted[s], 1)
                        if kind == "A" and (layer, u, phase) in ((1, 1, 0), (2, 0, 2), (3, 0, 0)):
                            inv_std(s, kk, layer)
                    if what == "end":
                        s = arg
                        pool.wait_ge(negs_ready[s], nth(k, 2, 1))
                        if att:
                            pool.wait_ge(att_filled[s], nth(k - 1, NJ, POS[3, "X", 0]))
                        pool.nop(nofuse=True)
                        pool.tensor_copy(neg1[s][:], neg1_next[s][:]).then_inc(neg_moved[s], 1)
                        pool.tensor_copy(neg3[s][:], neg3_next[s][:]).then_inc(neg_moved[s], 1)

            def keep(s, k):
                pool.wait_ge(x_loaded[s], 16 * (k + 1))
                if not (isinstance(k, int) and k == 0):
                    pool.wait_ge(turn_drained, y0_count(s, k - 1))
                pool.nop(nofuse=True)
                pool.tensor_copy(x_keep[s][:], x_in[s][:]).then_inc(x_kept[s], 1)

            def init(s, k):
                pool.wait_ge(turn_drained, init_turn(s, k))
                pool.nop(nofuse=True)
                pool.tensor_copy(h_hi[s][:], h_feat[s][:]).then_inc(h_hi_ready[s], 1)
                pool.wait_ge(h_hi_ready[s], nth(k, 5, 0))
                pool.tensor_tensor(h_lo[s][:], h_feat[s][:], h_hi[s][:].bitcast(F32),
                                   ALU.subtract).then_inc(h_lo_ready[s], 1)

            def start():
                keep(0, 0)
                init(0, 0)

            def inv_std(s, kg, i):
                pool.wait_ge(veps_ready[s], nth(kg, 4, i))
                pool.tensor_tensor(rstd[s][:], veps[s][:], minus_half[:], ALU.pow).then_inc(rstd_ready[s], 1)

            def cut_terms(s, kg, layer):
                pool.wait_ge(att_drained[s], nth(kg, NJ, POS[layer, "P", GS - 1]))
                w = 2 * H if layer == 1 else 2
                src = terms[s][:] if layer == 1 else h2[s][:, :, D:L2C]
                to = parts[s] if layer == 1 else parts2[s]
                left = rest[s][:, :, 0:w]
                pool.nop(nofuse=True)
                pool.tensor_copy(to[:, :, 0, :], src).then_inc(cut_done[s], 1)
                pool.wait_ge(cut_done[s], nth(kg, 6, 2 * (layer - 1)))
                pool.tensor_tensor(left, src, to[:, :, 0, :], ALU.subtract).then_inc(rest_done[s], 1)
                pool.wait_ge(rest_done[s], nth(kg, 3, layer - 1))
                pool.nop(nofuse=True)
                pool.tensor_copy(to[:, :, 1, :], left).then_inc(cut_done[s], 1)
                pool.wait_ge(cut_done[s], nth(kg, 6, 2 * (layer - 1) + 1))
                pool.tensor_tensor(to[:, :, 2, :], left, to[:, :, 1, :], ALU.subtract).then_inc(parts_ready[s], 1)

            start()
            body(0, True, False)
            with pool.Fori(1, NB - 1) as k:
                body(k, True, True)
            body(NB - 1, True, True, more=False)
            body(NB, False, True)

        @block.tensor
        def _(pe):
            def three_pass(o, w_hi, w_lo, x_hi, x_lo, start, stop):
                pe.matmul(o, w_hi, x_hi, start=start, stop=False, skip_group_check=True)
                pe.matmul(o, w_hi, x_lo, start=False, stop=False, skip_group_check=True)
                return pe.matmul(o, w_lo, x_hi, start=False, stop=stop, skip_group_check=True)

            pe.wait_ge(ident_ready, 1)
            pe.wait_ge(weights_in, 16 * N_WEIGHTS)
            raws = {"ih": raw_ih, "hh": raw_hh, "p1": raw_p1, "p2": raw_p2, "p3": raw_p3}
            for q, (what, m, i) in enumerate(panels):
                bank = setup_bank[q % 2]
                if q >= 2:
                    pe.wait_ge(setup_drained, q - 1)
                if what == "turn":
                    for f in range(4):
                        if m in ("ih", "hh"):
                            kc, c = divmod(4 * i + f, 6)
                            src = raws[m][:, c, kc * P:(kc + 1) * P]
                        elif m == "w":
                            kc, c = divmod(f, KC)
                            src = raw_w[:, i, c, kc * P:(kc + 1) * P]
                        else:
                            kc, c = divmod(f, KC)
                            src = raws[m][:, c, kc * P:(kc + 1) * P]
                        last = pe.transpose(bank[:, f * P:(f + 1) * P], src, ident[:])
                elif what == "fold":
                    dc, nh = i
                    n0, n1 = ((0, 512), (512, G3))[nh]
                    for kc in range(KC):
                        last = pe.matmul(bank[:, 0:n1 - n0], wT[:, m, kc, dc * P:(dc + 1) * P],
                                         wihT[:, kc, n0:n1], start=(kc == 0), stop=(kc == KC - 1))
                else:
                    if m == "p1" and i == 0:
                        pe.wait_ge(vectors_in, 16 * N_VECTORS)
                        pe.wait_ge(setup_dve, 5)
                    w = 2 * H if m in ("p1", "bias") else 2
                    for kc in range(KC):
                        lhs = {"p1": p1T, "p2": p2T, "p3": raw_p3}.get(m)
                        lhs = b_wide[:, kc, :] if m == "bias" else lhs[:, kc, i * P:(i + 1) * P]
                        rhs = {"p2": a2_cols, "p3": a3_cols}.get(m)
                        rhs = a_block[:, kc, :] if m in ("p1", "bias") else rhs[:, :, kc]
                        last = pe.matmul(bank[:, 0:w], lhs, rhs, start=(kc == 0), stop=(kc == KC - 1))
                last.then_inc(setup_filled, 1)
            pe.wait_ge(setup_done, 1)

            def turn(bank, src):
                o = bank[:].rearrange("p (c t) -> p c t", c=KC)
                for c in range(KC):
                    for g in range(GS):
                        last = pe.transpose(o[:, c, g * P:(g + 1) * P], src[:, g, c * P:(c + 1) * P], ident[:])
                return last

            def body(k, gru, att, more=True):
                for part in order:
                    what, arg, kk, on = part_of(part, k, gru, att, more)
                    if not on:
                        continue
                    if what == "init":
                        init(arg, kk)
                    if what == "agg":
                        n, s = arg, arg % 2
                        if n < NS:
                            pe.wait_ge(x_kept[s], nth(kk, 1, 0))
                            pe.wait_ge(edges_ready[s], nth(kk, 1, 0))
                            node = x_keep[s]
                        else:
                            pe.wait_ge(turn_drained, nth(kk, TURN, n))
                            node = h_node[s]
                        pe.wait_ge(u_ready, kk * 6 + n)
                        o = bank3(agg_bank, KC)
                        for c in range(KC):
                            for g in range(GS):
                                last = pe.matmul(o[:, c, g * P:(g + 1) * P], node[:, g, c * P:(c + 1) * P],
                                                 edges[s][:, g, :], start=True, stop=True)
                        last.then_inc(agg_filled, 1)
                    if what == "gates_h":
                        n, c, gate = arg
                        s = n % 2
                        if gate == 0:
                            pe.wait_ge(h_lo_ready[s], nth(kk, 5, 2 * (n // 2)))
                            pe.wait_ge(pre_ready[c], kk * 6 + n)
                            pe.wait_ge(z_ready[c], kk * 6 + n)
                        bank, half = ((gates_rz[c], 0), (gates_rz[c], 1), (gates_ih[c], 1))[gate]
                        col = gate * D + c * P
                        for kc in range(KC):
                            last = three_pass(bank3(bank, 2)[:, half, :], whh_hi[:, kc, col:col + P],
                                              whh_lo[:, kc, col:col + P], h_hi[s][:, kc, :], h_lo[s][:, kc, :],
                                              start=(kc == 0 and gate != 1), stop=False)
                        if gate == 2:
                            last.then_inc(h_used[c], 1)
                    if what == "gates_u":
                        n, c, gate = arg
                        it = n // 2
                        if gate == 0:
                            pe.wait_ge(u_ready, nth(kk, 6, n))
                        bank, half = ((gates_rz[c], 0), (gates_rz[c], 1), (gates_ih[c], 0))[gate]
                        col = gate * D + c * P
                        for kc in range(KC):
                            last = three_pass(bank3(bank, 2)[:, half, :], wc_hi[:, it, kc, col:col + P],
                                              wc_lo[:, it, kc, col:col + P], u_hi[:, kc, :], u_lo[:, kc, :],
                                              start=False, stop=(kc == KC - 1))
                        if gate == 2:
                            last.then_inc(gates_filled[c], 1)
                    if what == "turn":
                        n, s = arg, arg % 2
                        count = turn5(kk) if n == SLOTS - 1 else nth(kk, TURN, n + 2)
                        pe.wait_ge(turn_drained, count - 1)
                        for c in range(KC):
                            pe.wait_ge(h_ready[c], nth(kk, 6, n))
                        o = bank3(turn_bank, GS)
                        for g in range(GS):
                            for c in range(KC):
                                last = pe.transpose(o[:, g, c * P:(c + 1) * P], h_feat[s][:, c, g * P:(g + 1) * P], ident[:])
                        last.then_inc(turn_filled, 1)
                    if what == "att" and arg[2] == 0:
                        s, j, _ = arg
                        if j:
                            pe.wait_ge(att_drained[s], kk * NJ + j)
                        content(s, kk, *CONTENT[j]).then_inc(att_filled[s], 1)

            def init(s, k):
                pe.wait_ge(x_kept[s], nth(k, 1, 0))
                if not (isinstance(k, int) and k == 0 and s == 0):
                    pe.wait_ge(turn_drained, init_turn(s, k) - 1)
                turn(turn_bank, x_keep[s]).then_inc(turn_filled, 1)

            def start():
                init(0, 0)

            def content(s, kg, layer, kind, u):
                bank = att_bank[s]
                if kind == "T":
                    pe.wait_ge(xn_ready[s], nth(kg, 3, layer - 1))
                    return turn(bank, xn[s])
                if kind == "P":
                    w_hi, w_lo, w = {1: (p1_hi, p1_lo, L1C), 2: (p2_hi, p2_lo, L2C), 3: (p3_hi, p3_lo, L2C)}[layer]
                    for kc in range(KC):
                        a_hi, a_lo = (t[s][:, kc, u * P:(u + 1) * P] for t in (xT_hi, xT_lo))
                        last = three_pass(bank[:, 0:w], a_hi, a_lo, w_hi[:, kc, :], w_lo[:, kc, :],
                                          start=(kc == 0), stop=(kc == KC - 1))
                    return last
                if kind == "R":
                    pe.wait_ge(parts_ready[s], nth(kg, 3, layer - 1))
                    pe.nop(nofuse=True)
                    w = 48 if layer == 1 else 6
                    src = parts[s] if layer == 1 else parts2[s]
                    o = bank[0:w, 0:P].bitcast(BF16).rearrange("r (g i) -> r g i", g=GS)
                    for g in range(GS):
                        last = pe.transpose(o[:, g, :], src[:, g].rearrange("p a b -> p (a b)"), ident_b[:])
                    return last
                if kind == "X" and layer == 1:
                    pe.wait_ge(neg_moved[s], nth(kg, 2, 1))
                    g, half = divmod(u, 2)
                    row = rows[s][0:48, g, :]
                    pe.matmul(bank[:], ident_b[:], neg1[s][:, g, :].unsqueeze(1).to_broadcast([P, 4, P]),
                              start=True, stop=False, skip_group_check=True)
                    pe.matmul(bank[:], row, sel16[:, 4 * half:4 * half + 4, :].rearrange("r a b -> r (a b)"),
                              start=False, stop=False, skip_group_check=True)
                    for q in range(4):
                        last = pe.matmul(bank[:, q * P:(q + 1) * P], sel16[:, H + 4 * half + q, :], row,
                                         start=False, stop=(q == 3), skip_group_check=True)
                    return last
                if kind == "X":
                    pe.wait_ge(neg_moved[s], nth(kg, 2, 1))
                    for g in range(GS):
                        o = bank[:, g * P:(g + 1) * P]
                        row = rows[s][0:6, g, :]
                        if layer == 2:
                            pe.matmul(o, neg3[s][:, g, :], ident_b[:], start=(g == 0), stop=False, skip_group_check=True)
                        else:
                            pe.matmul(o, ident_b[:], neg3[s][:, g, :], start=(g == 0), stop=False, skip_group_check=True)
                        free, part = (0, 1) if layer == 2 else (1, 0)
                        pe.matmul(o, sel2[:, free, :], row, start=False, stop=False, skip_group_check=True)
                        last = pe.matmul(o, row, sel2[:, part, :], start=False, stop=(g == 1), skip_group_check=True)
                    return last
                if kind == "Y":
                    if layer == 1:
                        pe.wait_ge(prob_ready[s], nth(kg, 5, u))
                        for q in range(4):
                            last = pe.transpose(bank[:, q * P:(q + 1) * P], prob[s][u % 2][:, q, :], ident[:])
                    else:
                        pe.wait_ge(summed[s], nth(kg, 2, 1))
                        for g in range(GS):
                            last = pe.transpose(bank[:, g * P:(g + 1) * P], prob[s][0][:, g, :], ident[:])
                    return last
                if layer == 1:
                    for q in range(H):
                        last = pe.matmul(bank[:, q * (C + 1):(q + 1) * (C + 1)], probT[s][:, q, :],
                                         h1[s][:, u, q, :], start=True, stop=True)
                    return last
                if layer == 2:
                    pe.wait_ge(prob_ready[s], nth(kg, 5, 4))
                for g in range(GS):
                    lhs = prob[s][0][:, g, :] if layer == 2 else probT[s][:, g, :]
                    last = pe.matmul(bank[:, g * D:(g + 1) * D], lhs, h2[s][:, g, 0:D], start=True, stop=True)
                return last

            start()
            body(0, True, False)
            with pe.Fori(1, NB - 1) as k:
                body(k, True, True)
            body(NB - 1, True, True, more=False)
            body(NB, False, True)

        @block.scalar
        def _(act):
            with nc.allow_non_contiguous_dma(reason="vectors of the setup, once"):
                act.dma_start(bi[:], b_ih.rearrange("(c p) -> p c", p=P)).then_inc(vectors_in, 16)
                act.dma_start(bh[:], b_hh.rearrange("(c p) -> p c", p=P)).then_inc(vectors_in, 16)
                act.dma_start(b_col[:], proj_b.rearrange("(c p) -> p c", p=P)).then_inc(vectors_in, 16)
                act.dma_start(bias1[:, 0:D], proj_b.rearrange("(a d) -> a d", a=1).to_broadcast([P, D])).then_inc(vectors_in, 16)
                act.dma_start(a2_cols[:].rearrange("p w c -> p (w c)"), a2.rearrange("(w p) o -> p (w o)", p=P)).then_inc(vectors_in, 16)
                act.dma_start(a3_cols[:].rearrange("p w c -> p (w c)"), a3.rearrange("(w p) o -> p (w o)", p=P)).then_inc(vectors_in, 16)
                act.wait_ge(block_zero, 1)
                for side, vec in enumerate((a_fst, a_snd)):
                    for q in range(H):
                        c, row = divmod(q * C, P)
                        act.dma_start(a_block[row:row + C, c, side * H + q:side * H + q + 1],
                                      vec[q:q + 1, :].rearrange("a c -> c a")).then_inc(vectors_in, 16)
            act.wait_ge(setup_done, 1)

            def body(k, gru, att, more=True):
                for part in order:
                    what, arg, kk, on = part_of(part, k, gru, att, more)
                    if not on:
                        continue
                    if what == "init":
                        init(arg, kk)
                    if what == "agg":
                        act.wait_ge(agg_filled, nth(kk, 6, arg))
                        act.activation(flat(u_hi), agg_bank[:], ACT.Copy).then_inc(u_hi_ready, 1)
                    if what == "gates_u" and arg[2] == 2:
                        n, c, _ = arg
                        act.wait_ge(gates_filled[c], nth(kk, 6, n))
                        act.activation(tr[c][:], bank3(gates_rz[c], 2)[:, 0, :], ACT.Tanh,
                                       bias=half_b[:, c:c + 1], scale=0.5)
                        act.activation(hn[c][:], bank3(gates_ih[c], 2)[:, 1, :], ACT.Identity,
                                       bias=half_bh[:, 4 + c:5 + c], scale=0.5).then_inc(r_hn_ready[c], 1)
                        act.wait_ge(e_ready[c], kk * 6 + n)
                        act.activation(tz[c][:], bank3(gates_rz[c], 2)[:, 1, :], ACT.Tanh,
                                       bias=half_b[:, KC + c:KC + c + 1], scale=0.5).then_inc(z_ready[c], 1)
                    if what == "gru":
                        n, c = arg
                        act.wait_ge(pre_ready[c], nth(kk, 6, n))
                        act.activation(nn[c][:], pre[c][:], ACT.Tanh, bias=bi[:, 4 + c:5 + c]).then_inc(n_ready[c], 1)
                    if what == "turn" and arg < SLOTS - NS:
                        act.wait_ge(turn_filled, nth(kk, TURN, arg + 2))
                        act.activation(flat(h_node[arg % 2]), turn_bank[:], ACT.Copy).then_inc(turn_drained, 1)
                    if what == "att":
                        attend(*arg[:2], kk, *CONTENT[arg[1]], arg[2])

            def attend(s, j, kg, layer, kind, u, phase):
                bank = att_bank[s]
                if phase == 0 and (kind in "TRX" or (kind == "P" and layer > 1) or (kind == "Y" and u % 2 == 0)):
                    act.wait_ge(att_filled[s], nth(kg, NJ, j))
                if phase == 0 and kind == "T":
                    act.activation(flat(xT_hi[s]), bank[:], ACT.Copy).then_inc(xT_hi_ready[s], 1)
                if phase == 0 and kind == "P" and layer > 1:
                    act.activation(h2[s][:, u, :], bank[:, 0:L2C], ACT.Copy).then_inc(att_drained[s], 1)
                if phase == 0 and kind == "R":
                    w = 48 if layer == 1 else 6
                    act.activation(flat(rows[s][0:w]), bank[0:w, 0:P].bitcast(BF16), ACT.Copy).then_inc(att_drained[s], 1)
                if phase == 0 and kind == "X":
                    w = 4 if layer == 1 else GS
                    e = flat(prob[s][u % 2][:, 0:w, :])
                    act.activation(e, bank[:, 0:w * P], ACT.Copy, scale=SLOPE).then_inc(scaled_ready[s], 1)
                if phase == 0 and kind == "Y" and u % 2 == 0:
                    w = 4 if layer == 1 else GS
                    act.activation(flat(probT[s][:, 0:w, :]), bank[:, 0:w * P], ACT.Copy).then_inc(att_drained[s], 1)
                if phase == 2 and kind == "X" and layer == 1:
                    act.wait_ge(shifted[s], nth(kg, 4, u))
                    e = prob[s][u % 2][:]
                    act.activation(e, e, ACT.Exp).then_inc(prob_ready[s], 1)
                if phase == 1 and kind == "X" and layer > 1:
                    act.wait_ge(mtop_ready[s], nth(kg, 6, 2 + layer))
                    act.wait_ge(att_drained[s], nth(kg, NJ, j))
                    for g in range(GS):
                        last = act.activation(prob[s][0][:, g, :], prob[s][0][:, g, :], ACT.Exp,
                                              bias=mtop[s][0][:, g:g + 1], accum_out=zsum[s][:, g:g + 1])
                    last.then_inc(summed[s], 1)
                if phase == 1 and kind == "A" and layer == 2:
                    act.wait_ge(below_ready[s], nth(kg, 1, 0))
                    act.activation(below[s][:], below[s][:], ACT.Exp).then_inc(elu_ready[s], 1)

            def init(s, k):
                act.wait_ge(turn_filled, init_turn(s, k))
                act.activation(flat(h_feat[s]), turn_bank[:], ACT.Copy).then_inc(turn_drained, 1)

            def start():
                init(0, 0)

            start()
            body(0, True, False)
            with act.Fori(1, NB - 1) as k:
                body(k, True, True)
            body(NB - 1, True, True, more=False)
            body(NB, False, True)

        @block.vector
        def _(dve):
            dve.memset(a_block[:], 0.0).then_inc(block_zero, 1)
            for s in range(NS):
                last = dve.memset(h1[s][:], 1.0)
            last.then_inc(setup_dve, 1)
            dve.wait_ge(ident_ready, 1)
            dve.tensor_copy(ident_b[:], ident[:]).then_inc(setup_dve, 1)
            dve.tensor_tensor(pick16[:], ident[0:48, 0:16], ident[0:48, 16:32], ALU.add)
            dve.tensor_tensor(pick2[:], ident[0:6, 0:2], ident[0:6, 2:4], ALU.add).then_inc(setup_dve, 1)
            dve.wait_ge(setup_dve, 3)
            dve.tensor_tensor(pick16[:], pick16[:], ident[0:48, 32:48], ALU.add)
            dve.tensor_tensor(pick2[:], pick2[:], ident[0:6, 4:6], ALU.add).then_inc(setup_dve, 1)
            dve.wait_ge(setup_dve, 4)
            dve.tensor_copy(sel16[:], pick16[:].unsqueeze(2).to_broadcast([48, 16, P]))
            dve.tensor_copy(sel2[:], pick2[:].unsqueeze(2).to_broadcast([6, 2, P]))
            dve.wait_ge(vectors_in, 16 * N_VECTORS)
            dve.tensor_copy(b_wide[:], b_col[:].unsqueeze(2).to_broadcast([P, KC, P])).then_inc(setup_dve, 1)
            dve.tensor_tensor(bsum[:], bi[:], bh[:], ALU.add).then_inc(setup_dve, 1)
            dve.tensor_scalar(half_bh[:], bh[:], 0.5, None, ALU.mult)
            dve.wait_ge(setup_dve, 6)

            def two_parts(hi, lo, src, n):
                dve.tensor_copy(hi, src).then_inc(setup_hi, 1)
                dve.wait_ge(setup_hi, n)
                return dve.tensor_tensor(lo, src, hi.bitcast(F32), ALU.subtract)

            dve.wait_ge(weights_in, 16 * N_WEIGHTS)
            two_parts(p1_hi[:, :, 0:D], p1_lo[:, :, 0:D], raw_p1[:], 1)
            two_parts(p2_hi[:, :, 0:D], p2_lo[:, :, 0:D], raw_p2[:], 2)
            pairs = 2
            for q, (what, m, i) in enumerate(panels):
                bank = setup_bank[q % 2]
                dve.wait_ge(setup_filled, q + 1)
                if what == "turn" and m in ("ih", "w", "p1", "p2"):
                    to = {"ih": wihT, "w": wT, "p1": p1T, "p2": p2T}[m]
                    if m == "ih":
                        to = to[:].rearrange("p k e -> p (k e)")[:, i * 512:(i + 1) * 512]
                    elif m == "w":
                        to = to[:, i].rearrange("p k e -> p (k e)")
                    else:
                        to = to[:].rearrange("p k e -> p (k e)")
                    dve.tensor_copy(to, bank[:]).then_inc(setup_drained, 1)
                    continue
                if what == "turn" and m == "hh":
                    hi, lo = (t[:].rearrange("p k e -> p (k e)")[:, i * 512:(i + 1) * 512] for t in (whh_hi, whh_lo))
                    src = bank[:]
                elif what == "turn":
                    hi, lo, src = p3_hi[:, :, 0:D], p3_lo[:, :, 0:D], bank3(bank, KC)
                elif what == "fold":
                    dc, nh = i
                    n0, n1 = ((0, 512), (512, G3))[nh]
                    hi, lo, src = wc_hi[:, m, dc, n0:n1], wc_lo[:, m, dc, n0:n1], bank[:, 0:n1 - n0]
                elif m == "bias":
                    dve.tensor_copy(bias1[:, D:L1C], bank[:, 0:2 * H]).then_inc(setup_drained, 1)
                    continue
                else:
                    hi, lo, w = {"p1": (p1_hi, p1_lo, L1C), "p2": (p2_hi, p2_lo, L2C), "p3": (p3_hi, p3_lo, L2C)}[m]
                    hi, lo, src = hi[:, i, D:w], lo[:, i, D:w], bank[:, 0:w - D]
                pairs += 1
                two_parts(hi, lo, src, pairs).then_inc(setup_drained, 1)
            dve.wait_ge(setup_drained, len(panels))
            dve.tensor_scalar(half_b[:], bsum[:], 0.5, None, ALU.mult).then_inc(setup_done, 1)

            def norm_stats(s, kg, i, src):
                if i == 0:
                    dve.wait_ge(turn_drained, y0_count(s, kg))
                elif i == 3:
                    dve.wait_ge(att_drained[s], nth(kg, NJ, NJ - 1))
                else:
                    dve.wait_ge(y_ready[s], nth(kg, 2, i - 1))
                for g in range(GS):
                    last = dve.bn_stats(stats[s][:, g, :], src[:, g, :])
                last.then_inc(stats_ready[s], 1)
                dve.wait_ge(stats_ready[s], nth(kg, 4, i))
                dve.nop(nofuse=True)
                for g in range(GS):
                    last = dve.bn_aggr(mv[s][:, g, :], stats[s][:, g, :])
                last.then_inc(mv_ready[s], 1)
                dve.wait_ge(mv_ready[s], nth(kg, 4, i))
                dve.tensor_scalar(veps[s][:], mv[s][:, :, 1], EPS, None, ALU.add).then_inc(veps_ready[s], 1)

            def norm_apply(s, kg, i, src):
                dve.wait_ge(rstd_ready[s], nth(kg, 4, i))
                if i == 3:
                    dve.wait_ge(stored[s], 16 * kg + 1)
                to = result[s] if i == 3 else xn[s]
                for g in range(GS):
                    last = dve.tensor_scalar(to[:, g, :], src[:, g, :], mv[s][:, g, 0:1], rstd[s][:, g:g + 1],
                                             ALU.subtract, ALU.mult)
                last.then_inc(result_ready[s] if i == 3 else xn_ready[s], 1)

            def body(k, gru, att, more=True):
                for part in order:
                    what, arg, kk, on = part_of(part, k, gru, att, more)
                    if not on:
                        continue
                    if what == "edges":
                        find_edges(arg, kk)
                    if what == "negs":
                        s = arg
                        dve.wait_ge(adj_loaded[s], 16 * (kk + 1))
                        dve.wait_ge(neg_moved[s], kk * 2)
                        dve.tensor_scalar(neg1_next[s][:], adj_in[s][:], 1, MASKED, ALU.not_equal, ALU.mult).then_inc(negs_ready[s], 1)
                        dve.tensor_scalar(neg3_next[s][:], adj_in[s][:], 0, MASKED, ALU.is_le, ALU.mult).then_inc(negs_ready[s], 1)
                    if what == "norm0":
                        norm_stats(arg, kk, 0, y0[arg])
                    if what == "norm0b":
                        norm_apply(arg, kk, 0, y0[arg])
                    if what == "agg":
                        dve.wait_ge(u_hi_ready, nth(kk, 6, arg))
                        dve.tensor_tensor(flat(u_lo), agg_bank[:], flat(u_hi).bitcast(F32), ALU.subtract).then_inc(u_ready, 1)
                    if what == "gates_u" and arg[2] == 2:
                        n, c, _ = arg
                        dve.wait_ge(r_hn_ready[c], nth(kk, 6, n))
                        dve.scalar_tensor_tensor(pre[c][:], tr[c][:], 1.0, hn[c][:], ALU.add, ALU.mult).then_inc(q_ready[c], 1)
                        dve.wait_ge(q_ready[c], nth(kk, 6, n))
                        dve.tensor_tensor(pre[c][:], bank3(gates_ih[c], 2)[:, 0, :], pre[c][:], ALU.add).then_inc(pre_ready[c], 1)
                    if what == "gru":
                        n, c = arg
                        s = n % 2
                        dve.wait_ge(d_ready[c], nth(kk, 6, n))
                        dve.wait_ge(z_ready[c], nth(kk, 6, n))
                        dve.scalar_tensor_tensor(dd[c][:], tz[c][:], 1.0, dd[c][:], ALU.add, ALU.mult).then_inc(e_ready[c], 1)
                        dve.wait_ge(e_ready[c], nth(kk, 6, n))
                        dve.scalar_tensor_tensor(h_feat[s][:, c, :], dd[c][:], 0.5, nn[c][:], ALU.mult, ALU.add).then_inc(h_ready[c], 1)
                    if what == "turn" and arg >= SLOTS - NS:
                        s = arg % 2
                        dve.wait_ge(turn_filled, y0_count(s, kk))
                        dve.tensor_tensor(flat(y0[s]), turn_bank[:], flat(x_keep[s]), ALU.add).then_inc(turn_drained, 1)
                    if what == "att":
                        s, j, phase = arg
                        (attend if phase == 0 else attend_later)(s, kk, j, *CONTENT[j], phase)

            def find_edges(s, k):
                dve.wait_ge(adj_loaded[s], 16 * (k + 1))
                dve.tensor_scalar(edges[s][:], adj_in[s][:], 0, None, ALU.not_equal).then_inc(edges_ready[s], 1)

            def start():
                find_edges(0, 0)

            def attend(s, kg, j, layer, kind, u, phase):
                bank = att_bank[s]
                filled = nth(kg, NJ, j)
                if kind == "T":
                    dve.wait_ge(xT_hi_ready[s], nth(kg, 3, layer - 1))
                    dve.tensor_tensor(xT_lo[s][:].rearrange("p c t -> p (c t)"), bank[:],
                                      xT_hi[s][:].rearrange("p c t -> p (c t)").bitcast(F32), ALU.subtract).then_inc(att_drained[s], 1)
                if kind == "P" and layer == 1:
                    dve.wait_ge(att_filled[s], filled)
                    dve.tensor_tensor(h1[s][:, u, :, 0:C], bank[:, 0:D].rearrange("p (h c) -> p h c", h=H),
                                      bias1[:, 0:D].rearrange("p (h c) -> p h c", h=H), ALU.add)
                    last = dve.tensor_tensor(terms[s][:, u, :], bank[:, D:L1C], bias1[:, D:L1C], ALU.add)
                    last.then_inc(att_drained[s], 1)
                if kind == "X":
                    n, w = (4, 4) if layer == 1 else (GS, GS)
                    i = u if layer == 1 else 2 + layer
                    tp, mt = top[s][u % 2][:, 0:n], mtop[s][u % 2][:, 0:n]
                    e = prob[s][u % 2][:, 0:w, :]
                    b = bank[:, 0:w * P].rearrange("p (a b) -> p a b", a=w)
                    dve.wait_ge(scaled_ready[s], nth(kg, 6, i))
                    dve.tensor_reduce(tp, b, AX.X, ALU.max).then_inc(top_ready[s], 1)
                    dve.tensor_tensor(e, b, e, ALU.max).then_inc(att_drained[s], 1)
                    dve.wait_ge(top_ready[s], nth(kg, 6, i))
                    if layer == 1:
                        dve.scalar_tensor_tensor(mt, tp, SLOPE, tp, ALU.mult, ALU.max).then_inc(mtop_ready[s], 1)
                    else:
                        dve.tensor_scalar(rz[s][:, 0:n], tp, -1.0, None, ALU.mult).then_inc(rz_ready[s], 1)
                        dve.wait_ge(rz_ready[s], nth(kg, 6, (2, 4)[layer - 2]))
                        dve.scalar_tensor_tensor(mt, tp, -SLOPE, rz[s][:, 0:n], ALU.mult, ALU.min).then_inc(mtop_ready[s], 1)
                if kind == "Y" and u % 2 == 1:
                    dve.wait_ge(att_filled[s], filled)
                    dve.tensor_copy(probT[s][:, 4:8, :].rearrange("p a b -> p (a b)"), bank[:]).then_inc(att_drained[s], 1)
                if kind == "A" and layer == 1:
                    dve.wait_ge(att_filled[s], filled)
                    o = bank[:, 0:H * (C + 1)].rearrange("p (h c) -> p h c", h=H)
                    dve.reciprocal(rz[s][:], o[:, :, C]).then_inc(rz_ready[s], 1)
                    dve.wait_ge(rz_ready[s], nth(kg, 6, u))
                    dve.tensor_tensor(y[s][:, u].rearrange("p (h c) -> p h c", h=H), o[:, :, 0:C],
                                      rz[s][:].unsqueeze(2).to_broadcast([P, H, C]), ALU.mult).then_inc(att_drained[s], 1)
                    if u == 1:
                        dve.wait_ge(att_drained[s], filled)
                        dve.tensor_tensor(y[s][:], y[s][:], xn[s][:], ALU.add).then_inc(y_ready[s], 1)
                        norm_stats(s, kg, 1, y[s])
                if kind == "A" and layer == 2:
                    dve.wait_ge(att_filled[s], filled)
                    dve.tensor_scalar(below[s][:].rearrange("p g d -> p (g d)"), bank[:], 0.0, None, ALU.min).then_inc(below_ready[s], 1)
                if kind == "A" and layer == 3:
                    dve.wait_ge(att_filled[s], filled)
                    dve.wait_ge(rz_ready[s], nth(kg, 6, 5))
                    for g in range(GS):
                        last = dve.scalar_tensor_tensor(y[s][:, g, :], bank[:, g * D:(g + 1) * D], rz[s][:, g:g + 1],
                                                        xn[s][:, g, :], ALU.mult, ALU.add)
                    last.then_inc(att_drained[s], 1)
                    norm_stats(s, kg, 3, y[s])

            def attend_later(s, kg, j, layer, kind, u, phase):
                bank = att_bank[s]
                if kind == "X" and layer > 1 and phase == 2:
                    dve.wait_ge(summed[s], nth(kg, 2, layer - 2))
                    dve.reciprocal(rz[s][:, 0:GS], zsum[s][:]).then_inc(rz_ready[s], 1)
                    if layer == 2:
                        dve.wait_ge(rz_ready[s], nth(kg, 6, 3))
                        for g in range(GS):
                            last = dve.tensor_scalar(prob[s][0][:, g, :], prob[s][0][:, g, :], rz[s][:, g:g + 1], None, ALU.mult)
                        last.then_inc(prob_ready[s], 1)
                if kind == "A" and (layer, phase) in ((1, 1), (2, 3), (3, 1)):
                    norm_apply(s, kg, layer, y[s])
                if kind == "A" and (layer, phase) == (2, 2):
                    dve.wait_ge(elu_ready[s], nth(kg, 1, 0))
                    dve.scalar_tensor_tensor(flat(below[s]), bank[:], 0.0, flat(below[s]), ALU.max, ALU.add).then_inc(att_drained[s], 1)
                    dve.wait_ge(att_drained[s], nth(kg, NJ, j))
                    dve.scalar_tensor_tensor(y[s][:], below[s][:], -1.0, xn[s][:], ALU.add, ALU.add).then_inc(y_ready[s], 1)
                    norm_stats(s, kg, 2, y[s])

            start()
            body(0, True, False)
            with dve.Fori(1, NB - 1) as k:
                body(k, True, True)
            body(NB - 1, True, True, more=False)
            body(NB, False, True)


_INS = ["x", "adj", "L0_gnn_weight", "L0_gnn_w_ih", "L0_gnn_w_hh", "L0_gnn_b_ih", "L0_gnn_b_hh", "L1_gnn_proj_kernel",
        "L1_gnn_proj_bias", "L1_gnn_attn_fst", "L1_gnn_attn_snd", "L2_gnn_W", "L2_gnn_a", "L3_gnn_W", "L3_gnn_a"]


def kernel(**inputs):
    import numpy as _np
    import concourse.bacc as _bacc
    from concourse import mybir as _mybir
    from concourse.bass_utils import run_bass_kernel_spmd as _run

    nc = _bacc.Bacc("TRN2", target_bir_lowering=False, num_devices=1)
    arrays, args = {}, []
    for name in _INS:
        a = _np.ascontiguousarray(inputs[name])
        arrays[f"in_{name}"] = a
        args.append(nc.dram_tensor(f"in_{name}", a.shape, _mybir.dt.from_np(a.dtype), kind="ExternalInput").ap())
    shape = arrays["in_x"].shape
    args.append(nc.dram_tensor("out_0", shape, _mybir.dt.float32, kind="ExternalOutput").ap())
    graph_layers(nc, *args)
    r = _run(nc, [arrays], core_ids=[0])
    return r.results[0]["out_0"]
```

```python
from contextlib import ExitStack

import concourse.bass as bass
from concourse import mybir

ALU = mybir.AluOpType
ACT = mybir.ActivationFunctionType
AX = mybir.AxisListType
F32 = mybir.dt.float32
F32R = mybir.dt.float32r
BF16 = mybir.dt.bfloat16
I32 = mybir.dt.int32

P = 128
GS = 2
NS = 2
TOK = GS * P
MASKED = -9.0e15
SLOPE = 0.2
EPS = 1e-5
KC = 2
SLOTS = 6

LATE = {("gru", (SLOTS - 1, 1)), ("turn", SLOTS - 1)}
EARLY = {("keep", 0), ("edges", 0), ("init", 0)}

CONTENT = [(1, "T", 0), (1, "P", 0), (1, "P", 1), (1, "R", 0), (1, "X", 0), (1, "X", 1), (1, "Y", 0),
           (1, "X", 2), (1, "Y", 1), (1, "A", 0), (1, "X", 3), (1, "Y", 2), (1, "Y", 3), (1, "A", 1),
           (2, "T", 0), (2, "P", 0), (2, "P", 1), (2, "R", 0), (2, "X", 0), (2, "A", 0),
           (3, "T", 0), (3, "P", 0), (3, "P", 1), (3, "R", 0), (3, "X", 0), (3, "Y", 0), (3, "A", 0)]
NJ = len(CONTENT)
POS = {c: j for j, c in enumerate(CONTENT)}

ENGINES = ("pe", "act", "dve", "pool")
LAT = 190
TRANSPOSES = 427
WINDOW = 200
SEED, SHAKE = 4802, 4000


def tasks():
    T = {}

    def task(engine, part, spent, *after):
        T[engine, part] = (spent, [(b, back, lag + 50 if engine == "pe" and lag else lag) for b, back, lag in after])

    def of(engine, part, back=0, lag=LAT):
        return ((engine, part), back, lag)

    def slot_before(engine, kind, n, c, lag=LAT):
        n, back = (n - 1, 0) if n else (SLOTS - 1, 1)
        part = (kind, (n, c)) if kind == "gru" else (kind, (n, c, 2))
        return of(engine, part, back and part not in LATE, lag)

    turn_order = [("turn", SLOTS - 1), ("init", 1)] + [("turn", n) for n in range(SLOTS - 1)] + [("init", 0)]

    def empties(part):
        return "act" if part[0] == "turn" and part[1] < SLOTS - NS else "dve"

    for i, part in enumerate(turn_order):
        before = turn_order[i - 1]
        deps = [of(empties(before), before, i == 0)]
        kind, n = part
        if kind == "turn":
            deps += [of("dve", ("gru", (n, c)), part in LATE and ("gru", (n, c)) not in LATE) for c in range(KC)]
        elif n == 0:
            deps += [of("pe", ("gates_h", (SLOTS - NS, KC - 1, 2)), 0, 0)]
        task("pe", part, TRANSPOSES, *deps)
        if kind == "turn" and n < SLOTS - NS:
            task("act", part, 478, of("pe", part))
        elif kind == "turn":
            task("dve", part, 602, of("pe", part), *([of("dve", ("att", (0, POS[1, "A", 1], 0)), 0, 0)] if n == SLOTS - NS else []))
        else:
            task("act", part, 956, of("pe", part))
            task("dve", part, 602, of("act", part))
    for s in range(NS):
        task("dve", ("edges", s), 202, *([of("dve", ("agg", SLOTS - NS), 0, 0)] if s == 0 else []))
        task("dve", ("negs", s), 404, of("pool", ("end", s), 1))
        task("pool", ("keep", s), 1827, of("dve", ("turn", SLOTS - NS + s)))
        task("pool", ("end", s), 1946, of("dve", ("negs", s)), of("pe", ("att", (s, POS[3, "X", 0], 0))))
    for n in range(SLOTS):
        s = n % NS
        if n < NS:
            deps = [of("pool", ("keep", s), s == 0), of("dve", ("edges", s), s == 0)]
        else:
            deps = [of("act", ("turn", n - NS))]
        last, back = (n - 1, 0) if n else (SLOTS - 1, 1)
        task("pe", ("agg", n), 853, of("dve", ("agg", last), back), of("pe", ("gates_u", (last, KC - 1, 2)), back, 0), *deps)
        task("act", ("agg", n), 478, of("pe", ("agg", n)))
        task("dve", ("agg", n), 602, of("act", ("agg", n)))
        for c in range(KC):
            for gate in range(3):
                deps = []
                if gate == 0:
                    if n < NS:
                        deps += [of("dve", ("init", s), s == 0)]
                    else:
                        deps += [of("pool", ("split", (n - NS, k))) for k in range(KC)]
                    deps += [slot_before("dve", "gates_u", n, c), slot_before("act", "gates_u", n, c)]
                    deps += [of("pe", ("gates_h", (n, 0, 2)), 0, 0)] * c
                else:
                    deps += [of("pe", ("gates_h", (n, c, gate - 1)), 0, 0)]
                task("pe", ("gates_h", (n, c, gate)), 654, *deps)
                deps = [of("dve", ("agg", n)), of("pe", ("gates_h", (n, c, 2)), 0, 0)]
                if gate:
                    deps += [of("pe", ("gates_u", (n, c, gate - 1)), 0, 0)]
                elif c:
                    deps += [of("pe", ("gates_u", (n, 0, 2)), 0, 0)]
                task("pe", ("gates_u", (n, c, gate)), 654, *deps)
            late = ("gru", (n, c)) in LATE
            task("act", ("gates_u", (n, c, 2)), 1074, of("pe", ("gates_u", (n, c, 2))), slot_before("dve", "gru", n, c),
                 slot_before("act", "gru", n, c, 0))
            task("dve", ("gates_u", (n, c, 2)), 800, of("act", ("gates_u", (n, c, 2)), 0, LAT - 358), slot_before("dve", "gru", n, c, 0))
            task("act", ("gru", (n, c)), 400, of("dve", ("gates_u", (n, c, 2)), late))
            task("pool", ("gru", (n, c)), 687, of("act", ("gru", (n, c))))
            task("dve", ("gru", (n, c)), 800, of("pool", ("gru", (n, c))))
            if n < SLOTS - NS:
                task("pool", ("split", (n, c)), 1800, of("dve", ("gru", (n, c))), of("pe", ("gates_h", (n, KC - 1, 2))),
                     *([of("pool", ("split", (n, 0)), 0, 0)] * c))
    for s in range(NS):
        task("dve", ("norm0", s), 1220, of("dve", ("turn", SLOTS - NS + s), 0, 130))
        task("pool", ("norm0", s), 930, of("dve", ("norm0", s)))
        task("act", ("norm0b", s), 986, of("pool", ("norm0", s)))

        def att(engine, c, phase=0, lag=LAT):
            return of(engine, ("att", (s, POS[c], phase)), 0, lag)

        drain = of("dve", ("att", (s, NJ - 1, 0)), 1, LAT - 1100)
        for j, c in enumerate(CONTENT):
            layer, kind, u = c
            part = ("att", (s, j, 0))
            me = lambda engine, phase=0: of(engine, ("att", (s, j, phase)))
            name = lambda phase: ("att", (s, j, phase))
            deps = [drain]
            if kind == "T" and layer == 1:
                deps += [of("act", ("norm0b", s), s == 0)]
            if kind == "T" and layer == 2:
                deps += [att("act", (1, "A", 1), 1)]
            if kind == "T" and layer == 3:
                deps += [att("act", (2, "A", 0), 3)]
            if kind == "R":
                deps += [att("pool", (layer, "P", 1))]
            if kind == "X":
                deps += [of("pool", ("end", s), 1)]
            if kind == "Y":
                deps += [att("act", (layer, "X", u), 1)]
            if kind == "A" and layer == 2:
                deps += [att("dve", (2, "X", 0), 2)]
            spent = {"T": TRANSPOSES, "P": 680, "R": 110, "X": 650 if layer == 1 else 333,
                     "Y": TRANSPOSES if layer == 1 else TRANSPOSES // 2,
                     "A": 1640 if layer == 1 else 853}[kind]
            task("pe", part, spent, *deps)
            drain = me("dve")
            if kind == "T":
                task("act", part, 478, me("pe"))
                task("dve", part, 602, me("act"))
            elif kind == "P":
                if layer == 1:
                    task("dve", part, 420, me("pe"))
                else:
                    task("act", part, 266, me("pe"))
                    drain = me("act")
                if u == GS - 1:
                    task("pool", part, 1200 if layer == 1 else 1000, drain)
            elif kind == "R":
                task("act", part, 264, me("pe"))
                drain = me("act")
            elif kind == "X" and layer == 1:
                task("act", part, 478, me("pe"))
                task("dve", part, 1330, me("act"))
                drain = of("dve", part, 0, LAT - 730)
                task("act", name(1), 1172, me("dve"))
            elif kind == "X":
                task("act", part, 264, me("pe"))
                task("dve", part, 800, me("act"))
                drain = of("dve", part, 0, LAT - 460)
                task("act", name(1), 600, me("dve"))
                task("dve", name(2), 600 if layer == 2 else 80, me("act", 1))
            elif kind == "Y":
                task("act", part, 478 if layer == 1 else 264, me("pe"))
                drain = me("act")
            elif layer == 1:
                task("dve", part, 850 if u == 0 else 2800, me("pe"))
                drain = of("dve", part, 0, LAT if u == 0 else LAT - 1850)
                if u:
                    task("pool", part, 930, me("dve"))
                    task("act", name(1), 986, me("pool"))
            elif layer == 2:
                task("dve", part, 602, me("pe"))
                task("act", name(1), 520, me("dve"))
                task("dve", name(2), 2560, me("act", 1))
                task("pool", name(2), 930, me("dve", 2))
                task("act", name(3), 986, me("pool", 2))
                drain = me("dve", 2)
            else:
                task("dve", part, 2020, me("pe"), att("dve", (3, "X", 0), 2, 0))
                task("pool", part, 930, me("dve"))
                task("act", name(1), 986, me("pool"))
    return T


def urgency_of(T):
    followers = {t: [] for t in T}
    for t, (_, after) in T.items():
        for b, back, lag in after:
            if not back:
                followers[b].append((t, lag))
    level = {}

    def f(t):
        if t not in level:
            level[t] = T[t][0] + max([lag + f(u) for u, lag in followers[t]], default=0)
        return level[t]
    for t in T:
        f(t)
    return level


def alone(T):
    def on(part):
        return part in LATE or part[0] == "att" or part in (("norm0", 1), ("norm0b", 1))
    return {t: (spent, [a for a in after if on(a[0][1])]) for t, (spent, after) in T.items() if on(t[1])}


def frame(T, level, done, free):
    now, missing = {}, {}
    followers = {t: [] for t in T}
    for t, (_, after) in T.items():
        n = 0
        for b, back, lag in after:
            if not back:
                followers[b].append(t)
                n += 1
        missing[t] = n
    ready = {e: {} for e in free}

    def open_(t):
        at = 0
        for b, back, lag in T[t][1]:
            at = max(at, (done if back else now).get(b, 0) + lag)
        ready[t[0]][t] = at
    for t in T:
        if not missing[t]:
            open_(t)
    orders = {e: [] for e in free}
    for _ in range(len(T)):
        best = min((max(free[e], min(r.values())), e) for e, r in ready.items() if r)
        at, e = best
        t = max((t for t, a in ready[e].items() if a <= at + WINDOW), key=lambda t: level[t])
        at = max(free[e], ready[e].pop(t))
        now[t] = free[e] = at + T[t][0]
        orders[e].append(t[1])
        for u in followers[t]:
            missing[u] -= 1
            if not missing[u]:
                open_(u)
    return orders, now


def draws(seed):
    while True:
        seed = (seed * 1103515245 + 12345) % (1 << 31)
        yield seed / (1 << 31)


def make_schedule():
    T = tasks()
    draw = draws(SEED)
    level = {t: l + SHAKE * next(draw) for t, l in urgency_of(T).items()}
    done, free = {}, {e: 0 for e in ENGINES}
    for _ in range(3):
        orders, done = frame(T, level, done, free)
    rest = alone(T)
    last, _ = frame(rest, urgency_of(rest), {}, {e: 0 for e in ENGINES})
    return orders, last


def graph_layers(nc, x, adj, weight, w_ih, w_hh, b_ih, b_hh, proj, proj_b, a_fst, a_snd, W2, a2, W3, a3, out):
    B, N, D = x.shape
    L = weight.shape[0]
    H, C = a_fst.shape
    G3 = 3 * D
    NB = B // (GS * NS)
    L1C, L2C = D + 2 * H, D + 2
    assert (N, D, L, H * C) == (P, KC * P, SLOTS // NS, D)
    order, last_order = make_schedule()

    with ExitStack() as ctx:
        def sb(name, shape, dt=F32):
            return ctx.enter_context(nc.sbuf_tensor(name, shape, dt))

        def psum(name):
            return ctx.enter_context(nc.psum_tensor(name, [P, 512], F32))

        def sem(name):
            return ctx.enter_context(nc.semaphore(name))

        def sems(name, n=NS):
            return [sem(f"{name}_{i}") for i in range(n)]

        gates_rz = [psum(f"gates_rz_{c}") for c in range(KC)]
        gates_ih = [psum(f"gates_ih_{c}") for c in range(KC)]
        agg_bank = psum("agg_bank")
        turn_bank = psum("turn_bank")
        att_bank = [psum(f"att_bank_{s}") for s in range(NS)]

        whh_hi, whh_lo = (sb(n, [P, KC, G3], F32R) for n in ("whh_hi", "whh_lo"))
        wc_hi, wc_lo = (sb(n, [P, L, KC, G3], F32R) for n in ("wc_hi", "wc_lo"))
        p1_hi, p1_lo = (sb(n, [P, KC, L1C], F32R) for n in ("p1_hi", "p1_lo"))
        p2_hi, p2_lo = (sb(n, [P, KC, L2C], F32R) for n in ("p2_hi", "p2_lo"))
        p3_hi, p3_lo = (sb(n, [P, KC, L2C], F32R) for n in ("p3_hi", "p3_lo"))
        bias1 = sb("bias1", [P, L1C])
        bi, bh, bsum, half_b, half_bh = (sb(n, [P, 6]) for n in ("bi", "bh", "bsum", "half_b", "half_bh"))
        ident = sb("ident", [P, P])
        ident_b = sb("ident_b", [P, P], BF16)
        pick16 = sb("pick16", [48, 16])
        pick2 = sb("pick2", [6, 2])
        sel16 = sb("sel16", [48, 16, P], BF16)
        sel2 = sb("sel2", [6, 2, P], BF16)
        minus_half = sb("minus_half", [P, GS])

        x_in = [sb(f"x_in_{s}", [P, GS, D]) for s in range(NS)]
        adj_in = [sb(f"adj_in_{s}", [P, GS, P], I32) for s in range(NS)]
        x_keep = [sb(f"x_keep_{s}", [P, GS, D]) for s in range(NS)]
        edges = [sb(f"edges_{s}", [P, GS, P]) for s in range(NS)]
        neg1_next = [sb(f"neg1_next_{s}", [P, GS, P], BF16) for s in range(NS)]
        neg3_next = [sb(f"neg3_next_{s}", [P, GS, P], BF16) for s in range(NS)]
        h_feat = [sb(f"h_feat_{s}", [P, KC, TOK]) for s in range(NS)]
        h_hi = [sb(f"h_hi_{s}", [P, KC, TOK], F32R) for s in range(NS)]
        h_lo = [sb(f"h_lo_{s}", [P, KC, TOK], F32R) for s in range(NS)]
        h_node = [sb(f"h_node_{s}", [P, GS, D]) for s in range(NS)]
        u_hi, u_lo = (sb(n, [P, KC, TOK], F32R) for n in ("u_hi", "u_lo"))
        tr, tz, hn, pre, nn, dd = ([sb(f"{n}_{c}", [P, TOK]) for c in range(KC)]
                                   for n in ("tr", "tz", "hn", "pre", "nn", "dd"))
        y = [sb(f"y_{s}", [P, GS, D]) for s in range(NS)]
        y0 = [sb(f"y0_{s}", [P, GS, D]) for s in range(NS)]
        xn = [sb(f"xn_{s}", [P, GS, D]) for s in range(NS)]
        xT_hi = [sb(f"xT_hi_{s}", [P, KC, TOK], F32R) for s in range(NS)]
        xT_lo = [sb(f"xT_lo_{s}", [P, KC, TOK], F32R) for s in range(NS)]
        neg1 = [sb(f"neg1_{s}", [P, GS, P], BF16) for s in range(NS)]
        neg3 = [sb(f"neg3_{s}", [P, GS, P], BF16) for s in range(NS)]
        h1 = [sb(f"h1_{s}", [P, GS, H, C + 1]) for s in range(NS)]
        h2 = [sb(f"h2_{s}", [P, GS, L2C]) for s in range(NS)]
        terms = [sb(f"terms_{s}", [P, GS, 2 * H]) for s in range(NS)]
        rest = [sb(f"rest_{s}", [P, GS, 2 * H]) for s in range(NS)]
        parts = [sb(f"parts_{s}", [P, GS, 3, 2 * H], BF16) for s in range(NS)]
        parts2 = [sb(f"parts2_{s}", [P, GS, 3, 2], BF16) for s in range(NS)]
        rows = [sb(f"rows_{s}", [48, GS, P], BF16) for s in range(NS)]
        prob = [[sb(f"prob_{s}_{i}", [P, 4, P]) for i in range(2)] for s in range(NS)]
        mtop = [[sb(f"mtop_{s}_{i}", [P, 4]) for i in range(2)] for s in range(NS)]
        probT = [sb(f"probT_{s}", [P, H, P]) for s in range(NS)]
        zsum = [sb(f"zsum_{s}", [P, GS]) for s in range(NS)]
        rz = [sb(f"rz_{s}", [P, H]) for s in range(NS)]
        below = [sb(f"below_{s}", [P, GS, D]) for s in range(NS)]
        stats = [[sb(f"stats{w}_{s}", [P, GS, 6]) for s in range(NS)] for w in range(2)]
        mv = [[sb(f"mv{w}_{s}", [P, GS, 2]) for s in range(NS)] for w in range(2)]
        veps, minus_mean, rstd, shift = ([[sb(f"{n}{w}_{s}", [P, GS]) for s in range(NS)] for w in range(2)]
                                         for n in ("veps", "minus_mean", "rstd", "shift"))
        result = [sb(f"result_{s}", [P, GS, D]) for s in range(NS)]
        raw_ih, raw_hh = (sb(n, [P, 6, D]) for n in ("raw_ih", "raw_hh"))
        raw_w = sb("raw_w", [P, L, KC, D])
        raw_p1, raw_p2, raw_p3, p1T, p2T = result[0], result[1], y[0], below[0], below[1]
        wihT = sb("wihT", [P, KC, G3])
        wT = sb("wT", [P, L, KC, D])
        a_block = sb("a_block", [P, KC, 2 * H])
        a2_cols, a3_cols = (sb(n, [P, 2, KC]) for n in ("a2_cols", "a3_cols"))
        b_col = sb("b_col", [P, KC])
        b_wide = sb("b_wide", [P, KC, P])

        ident_zero, ident_ready, block_zero, half_ready = (sem(n) for n in ("ident_zero", "ident_ready", "block_zero", "half_ready"))
        weight_in = {m: sem(f"weight_in_{m}") for m in ("ih", "w", "hh", "p1", "p2", "p3")}
        vectors_in = sem("vectors_in")
        setup_filled, setup_copied, setup_split, setup_dve, setup_hi, setup_done = (
            sem(n) for n in ("setup_filled", "setup_copied", "setup_split", "setup_dve", "setup_hi", "setup_done"))
        x_loaded, adj_loaded, x_kept, edges_ready, negs_ready = (sems(n) for n in ("x_loaded", "adj_loaded", "x_kept", "edges_ready", "negs_ready"))
        gates_filled, h_used, r_hn_ready, z_ready, q_ready, pre_ready, n_ready, d_ready, e_ready, h_ready = (
            sems(n, KC) for n in ("gates_filled", "h_used", "r_hn_ready", "z_ready", "q_ready", "pre_ready",
                                  "n_ready", "d_ready", "e_ready", "h_ready"))
        h_hi_ready, h_lo_ready, x_split = sems("h_hi_ready"), sems("h_lo_ready"), sems("x_split")
        agg_filled, u_hi_ready, u_ready = sem("agg_filled"), sem("u_hi_ready"), sem("u_ready")
        turn_filled, turn_drained = sem("turn_filled"), sem("turn_drained")
        neg_moved = sems("neg_moved")
        att_filled, att_drained, xT_hi_ready, cut_done, rest_done, parts_ready = (
            sems(n) for n in ("att_filled", "att_drained", "xT_hi_ready", "cut_done", "rest_done", "parts_ready"))
        scaled_ready, mtop_ready, summed, prob_ready, rz_ready = (
            sems(n) for n in ("scaled_ready", "mtop_ready", "summed", "prob_ready", "rz_ready"))
        below_ready, elu_ready, y_ready, y0n_ready, xn_ready, result_ready, stored = (
            sems(n) for n in ("below_ready", "elu_ready", "y_ready", "y0n_ready", "xn_ready", "result_ready", "stored"))
        stats_ready, mv_ready, veps_ready, rstd_ready, shift_ready = (
            [sems(f"{n}{w}") for w in range(2)] for n in ("stats_ready", "mv_ready", "veps_ready", "rstd_ready", "shift_ready"))

        def nth(k, per, i):
            return k * per + (i + 1)

        def norm(kg, i):
            return (1, nth(kg, 3, i - 1)) if i else (0, nth(kg, 1, 0))

        x_v = x.rearrange("(k s g) n d -> k s n g d", s=NS, g=GS)
        adj_v = adj.rearrange("(k s g) n m -> k s n g m", s=NS, g=GS)
        out_v = out.rearrange("(k s g) n d -> k s n g d", s=NS, g=GS)

        TURN = 8

        def part_of(part, k, gru, att, more):
            kind, late = part[0], part in LATE
            if late or kind == "att" or part in (("norm0", 1), ("norm0b", 1)):
                return *part, k - 1, att
            if part in EARLY:
                return *part, k + 1, gru and more
            return *part, k, gru

        def turn5(kk):
            return nth(kk + 1, TURN, 0) - (isinstance(kk, int) and kk == NB - 1)

        def init_turn(s, k):
            return nth(k, TURN, 1) if s else (1 if isinstance(k, int) and k == 0 else k * TURN)

        def y0_count(s, k):
            return turn5(k) if s else nth(k, TURN, SLOTS)

        def flat(tile):
            return tile[:].rearrange("p a b -> p (a b)")

        def bank3(bank, a):
            return bank[:].rearrange("p (a b) -> p a b", a=a)

        panels = [("turn", "ih", i) for i in range(3)] + [("turn", "w", i) for i in range(L)]
        panels += [("turn", "hh", i) for i in range(3)] + [("turn", m, 0) for m in ("p1", "p2", "p3")]
        panels += [("fold", i, (dc, nh)) for i in range(L) for dc in range(KC) for nh in range(2)]
        panels += [("terms", m, dc) for m in ("p1", "p2", "p3") for dc in range(KC)] + [("terms", "bias", 0)]
        setup_bank = gates_rz + gates_ih + [agg_bank] + att_bank
        FIRST_FOLD, FIRST_TERMS = panels.index(("fold", 0, (0, 0))), panels.index(("terms", "p1", 0))
        N_VECTORS = 6 + 2 * H

        def copied(panel):
            return panel[0] == "turn" and panel[1] in ("ih", "w", "p1", "p2")

        def emptied(q):
            same = sum(copied(p) == copied(panels[q]) for p in panels[:q + 1])
            return (setup_copied if copied(panels[q]) else setup_split), same

        block = ctx.enter_context(nc.Block())

        @block.sync
        def _(sp):
            def load(k):
                for s in range(NS):
                    if not (isinstance(k, int) and k == 0):
                        sp.wait_ge(x_kept[s], k)
                        sp.nop(nofuse=True)
                        sp.wait_ge(edges_ready[s], k)
                        sp.nop(nofuse=True)
                        sp.wait_ge(negs_ready[s], k * 2)
                        sp.nop(nofuse=True)
                        sp.wait_ge(turn_filled, init_turn(s, k - 1))
                        sp.nop(nofuse=True)
                    sp.dma_start(x_in[s][:], x_v[k, s]).then_inc(x_loaded[s], 16)
                    sp.dma_start(adj_in[s][:], adj_v[k, s]).then_inc(adj_loaded[s], 16)

            def store(kg):
                for s in range(NS):
                    sp.wait_ge(result_ready[s], nth(kg, 1, 0))
                    sp.nop(nofuse=True)
                    sp.dma_start(out_v[kg, s], result[s][:]).then_inc(stored[s], 16)

            sp.dma_start(raw_ih[:], w_ih.rearrange("(c p) d -> p c d", p=P)).then_inc(weight_in["ih"], 16)
            sp.dma_start(raw_w[:], weight.rearrange("l (c p) d -> p l c d", p=P)).then_inc(weight_in["w"], 16)
            sp.dma_start(raw_hh[:], w_hh.rearrange("(c p) d -> p c d", p=P)).then_inc(weight_in["hh"], 16)
            load(0)
            for m, raw, src in (("p1", raw_p1, proj), ("p2", raw_p2, W2), ("p3", raw_p3, W3)):
                sp.dma_start(raw[:], src.rearrange("(c p) d -> p c d", p=P)).then_inc(weight_in[m], 16)
            with nc.allow_non_contiguous_dma(reason="vectors of the setup, once"):
                sp.dma_start(bi[:], b_ih.rearrange("(c p) -> p c", p=P)).then_inc(vectors_in, 16)
                sp.dma_start(bh[:], b_hh.rearrange("(c p) -> p c", p=P)).then_inc(vectors_in, 16)
                sp.dma_start(b_col[:], proj_b.rearrange("(c p) -> p c", p=P)).then_inc(vectors_in, 16)
                sp.dma_start(bias1[:, 0:D], proj_b.rearrange("(a d) -> a d", a=1).to_broadcast([P, D])).then_inc(vectors_in, 16)
                sp.dma_start(a2_cols[:].rearrange("p w c -> p (w c)"), a2.rearrange("(w p) o -> p (w o)", p=P)).then_inc(vectors_in, 16)
                sp.dma_start(a3_cols[:].rearrange("p w c -> p (w c)"), a3.rearrange("(w p) o -> p (w o)", p=P)).then_inc(vectors_in, 16)
                sp.wait_ge(block_zero, 1)
                for side, vec in enumerate((a_fst, a_snd)):
                    for q in range(H):
                        c, row = divmod(q * C, P)
                        sp.dma_start(a_block[row:row + C, c, side * H + q:side * H + q + 1],
                                      vec[q:q + 1, :].rearrange("a c -> c a")).then_inc(vectors_in, 16)
            load(1)
            with sp.Fori(1, NB - 1) as k:
                load(k + 1)
                store(k - 1)
            store(NB - 2)
            store(NB - 1)
            for s in range(NS):
                sp.wait_ge(stored[s], 16 * NB + 1)

        @block.gpsimd
        def _(pool):
            pool.memset(ident[:], 0.0).then_inc(ident_zero, 1)
            pool.wait_ge(ident_zero, 1)
            pool.affine_select(out=ident[:], in_=ident[:], compare_op=ALU.not_equal, fill=1.0, base=0,
                               pattern=[[-1, P]], channel_multiplier=1).then_inc(ident_ready, 1)
            pool.memset(minus_half[:], -0.5).then_inc(half_ready, 1)
            pool.wait_ge(half_ready, 1)
            for s in range(NS):
                pool.memset(rstd[0][s][:], 1.0).then_inc(stored[s], 1)

            def body(k, gru, att, more=True):
                for part in (order if gru else last_order)["pool"]:
                    what, arg, kk, on = part_of(part, k, gru, att, more)
                    if not on:
                        continue
                    if what == "keep":
                        keep(arg, kk)
                    if what == "norm0":
                        inv_std(arg, kk, 0)
                    if what == "gru":
                        n, c = arg
                        s = n % 2
                        pool.wait_ge(n_ready[c], nth(kk, 6, n))
                        pool.tensor_tensor(dd[c][:], h_feat[s][:, c, :], nn[c][:], ALU.subtract).then_inc(d_ready[c], 1)
                    if what == "split":
                        n, c = arg
                        s = n % 2
                        i = 2 * (n // 2) + c
                        pool.wait_ge(h_used[1], nth(kk, 6, n))
                        pool.wait_ge(h_ready[c], nth(kk, 6, n))
                        pool.nop(nofuse=True)
                        pool.tensor_copy(h_hi[s][:, c, :], h_feat[s][:, c, :]).then_inc(h_hi_ready[s], 1)
                        pool.wait_ge(h_hi_ready[s], nth(kk, 4, i))
                        pool.tensor_tensor(h_lo[s][:, c, :], h_feat[s][:, c, :], h_hi[s][:, c, :].bitcast(F32),
                                           ALU.subtract).then_inc(h_lo_ready[s], 1)
                    if what == "att":
                        s, j, phase = arg
                        layer, kind, u = CONTENT[j]
                        if (kind, u, phase) == ("P", GS - 1, 0):
                            cut_terms(s, kk, layer)
                        if kind == "A" and (layer, u, phase) in ((1, 1, 0), (2, 0, 2), (3, 0, 0)):
                            inv_std(s, kk, layer)
                    if what == "end":
                        s = arg
                        pool.wait_ge(negs_ready[s], nth(k, 2, 1))
                        if att:
                            pool.wait_ge(att_filled[s], nth(k - 1, NJ, POS[3, "X", 0]))
                        pool.nop(nofuse=True)
                        pool.tensor_copy(neg1[s][:], neg1_next[s][:]).then_inc(neg_moved[s], 1)
                        pool.tensor_copy(neg3[s][:], neg3_next[s][:]).then_inc(neg_moved[s], 1)

            def keep(s, k):
                pool.wait_ge(x_loaded[s], 16 * (k + 1))
                if not (isinstance(k, int) and k == 0):
                    pool.wait_ge(turn_drained, y0_count(s, k - 1))
                pool.nop(nofuse=True)
                pool.tensor_copy(x_keep[s][:], x_in[s][:]).then_inc(x_kept[s], 1)

            def start():
                keep(0, 0)

            def inv_std(s, kg, i):
                w, count = norm(kg, i)
                pool.wait_ge(veps_ready[w][s], count)
                pool.tensor_tensor(rstd[w][s][:], veps[w][s][:], minus_half[:], ALU.pow).then_inc(rstd_ready[w][s], 1)
                pool.wait_ge(rstd_ready[w][s], count)
                pool.tensor_tensor(shift[w][s][:], minus_mean[w][s][:], rstd[w][s][:], ALU.mult).then_inc(shift_ready[w][s], 1)

            def cut_terms(s, kg, layer):
                pool.wait_ge(att_drained[s], nth(kg, NJ, POS[layer, "P", GS - 1]))
                w = 2 * H if layer == 1 else 2
                src = terms[s][:] if layer == 1 else h2[s][:, :, D:L2C]
                to = parts[s] if layer == 1 else parts2[s]
                left = rest[s][:, :, 0:w]
                pool.nop(nofuse=True)
                pool.tensor_copy(to[:, :, 0, :], src).then_inc(cut_done[s], 1)
                pool.wait_ge(cut_done[s], nth(kg, 6, 2 * (layer - 1)))
                pool.tensor_tensor(left, src, to[:, :, 0, :], ALU.subtract).then_inc(rest_done[s], 1)
                pool.wait_ge(rest_done[s], nth(kg, 3, layer - 1))
                pool.nop(nofuse=True)
                pool.tensor_copy(to[:, :, 1, :], left).then_inc(cut_done[s], 1)
                pool.wait_ge(cut_done[s], nth(kg, 6, 2 * (layer - 1) + 1))
                pool.tensor_tensor(to[:, :, 2, :], left, to[:, :, 1, :], ALU.subtract).then_inc(parts_ready[s], 1)

            start()
            body(0, True, False)
            with pool.Fori(1, NB - 1) as k:
                body(k, True, True)
            body(NB - 1, True, True, more=False)
            body(NB, False, True)

        @block.tensor
        def _(pe):
            def three_pass(o, w_hi, w_lo, x_hi, x_lo, start, stop):
                pe.matmul(o, w_hi, x_hi, start=start, stop=False, skip_group_check=True)
                pe.matmul(o, w_hi, x_lo, start=False, stop=False, skip_group_check=True)
                return pe.matmul(o, w_lo, x_hi, start=False, stop=stop, skip_group_check=True)

            def turn(bank, src):
                o = bank[:].rearrange("p (c t) -> p c t", c=KC)
                for c in range(KC):
                    for g in range(GS):
                        last = pe.transpose(o[:, c, g * P:(g + 1) * P], src[:, g, c * P:(c + 1) * P], ident[:])
                return last

            def init(s, k):
                pe.wait_ge(x_loaded[s], 16 * (k + 1))
                if not (isinstance(k, int) and k == 0 and s == 0):
                    pe.wait_ge(turn_drained, init_turn(s, k) - 1)
                turn(turn_bank, x_in[s]).then_inc(turn_filled, 1)

            def start():
                init(0, 0)

            pe.wait_ge(ident_ready, 1)
            raws = {"ih": raw_ih, "hh": raw_hh, "p1": raw_p1, "p2": raw_p2, "p3": raw_p3}
            for q, (what, m, i) in enumerate(panels):
                bank = setup_bank[q % len(setup_bank)]
                if q >= len(setup_bank):
                    pe.wait_ge(*emptied(q - len(setup_bank)))
                if q == FIRST_FOLD:
                    pe.wait_ge(*emptied(panels.index(("turn", "w", L - 1))))
                    start()
                if q == FIRST_TERMS:
                    pe.wait_ge(*emptied(panels.index(("turn", "p2", 0))))
                if what == "turn":
                    pe.wait_ge(weight_in[m], 16)
                    for f in range(4):
                        if m in ("ih", "hh"):
                            kc, c = divmod(4 * i + f, 6)
                            src = raws[m][:, c, kc * P:(kc + 1) * P]
                        elif m == "w":
                            kc, c = divmod(f, KC)
                            src = raw_w[:, i, c, kc * P:(kc + 1) * P]
                        else:
                            kc, c = divmod(f, KC)
                            src = raws[m][:, c, kc * P:(kc + 1) * P]
                        last = pe.transpose(bank[:, f * P:(f + 1) * P], src, ident[:])
                elif what == "fold":
                    dc, nh = i
                    n0, n1 = ((0, 512), (512, G3))[nh]
                    for kc in range(KC):
                        last = pe.matmul(bank[:, 0:n1 - n0], wT[:, m, kc, dc * P:(dc + 1) * P],
                                         wihT[:, kc, n0:n1], start=(kc == 0), stop=(kc == KC - 1))
                else:
                    if m == "p1" and i == 0:
                        pe.wait_ge(vectors_in, 16 * N_VECTORS)
                        pe.wait_ge(setup_dve, 5)
                    w = 2 * H if m in ("p1", "bias") else 2
                    for kc in range(KC):
                        lhs = {"p1": p1T, "p2": p2T, "p3": raw_p3}.get(m)
                        lhs = b_wide[:, kc, :] if m == "bias" else lhs[:, kc, i * P:(i + 1) * P]
                        rhs = {"p2": a2_cols, "p3": a3_cols}.get(m)
                        rhs = a_block[:, kc, :] if m in ("p1", "bias") else rhs[:, :, kc]
                        last = pe.matmul(bank[:, 0:w], lhs, rhs, start=(kc == 0), stop=(kc == KC - 1))
                last.then_inc(setup_filled, 1)
            pe.wait_ge(setup_done, 1)

            def body(k, gru, att, more=True):
                for part in (order if gru else last_order)["pe"]:
                    what, arg, kk, on = part_of(part, k, gru, att, more)
                    if not on:
                        continue
                    if what == "init":
                        init(arg, kk)
                    if what == "agg":
                        n, s = arg, arg % 2
                        if n < NS:
                            pe.wait_ge(x_kept[s], nth(kk, 1, 0))
                            pe.wait_ge(edges_ready[s], nth(kk, 1, 0))
                            node = x_keep[s]
                        else:
                            pe.wait_ge(turn_drained, nth(kk, TURN, n))
                            node = h_node[s]
                        pe.wait_ge(u_ready, kk * 6 + n)
                        o = bank3(agg_bank, KC)
                        for c in range(KC):
                            for g in range(GS):
                                last = pe.matmul(o[:, c, g * P:(g + 1) * P], node[:, g, c * P:(c + 1) * P],
                                                 edges[s][:, g, :], start=True, stop=True)
                        last.then_inc(agg_filled, 1)
                    if what == "gates_h":
                        n, c, gate = arg
                        s = n % 2
                        if gate == 0:
                            if n < NS:
                                pe.wait_ge(turn_drained, init_turn(s, kk))
                            else:
                                pe.wait_ge(h_lo_ready[s], nth(kk, 4, 2 * (n // 2) - 1))
                            pe.wait_ge(pre_ready[c], kk * 6 + n)
                            pe.wait_ge(z_ready[c], kk * 6 + n)
                        bank, half = ((gates_rz[c], 0), (gates_rz[c], 1), (gates_ih[c], 1))[gate]
                        col = gate * D + c * P
                        for kc in range(KC):
                            last = three_pass(bank3(bank, 2)[:, half, :], whh_hi[:, kc, col:col + P],
                                              whh_lo[:, kc, col:col + P], h_hi[s][:, kc, :], h_lo[s][:, kc, :],
                                              start=(kc == 0 and gate != 1), stop=False)
                        if gate == 2:
                            last.then_inc(h_used[c], 1)
                    if what == "gates_u":
                        n, c, gate = arg
                        it = n // 2
                        if gate == 0:
                            pe.wait_ge(u_ready, nth(kk, 6, n))
                        bank, half = ((gates_rz[c], 0), (gates_rz[c], 1), (gates_ih[c], 0))[gate]
                        col = gate * D + c * P
                        for kc in range(KC):
                            last = three_pass(bank3(bank, 2)[:, half, :], wc_hi[:, it, kc, col:col + P],
                                              wc_lo[:, it, kc, col:col + P], u_hi[:, kc, :], u_lo[:, kc, :],
                                              start=False, stop=(kc == KC - 1))
                        if gate == 2:
                            last.then_inc(gates_filled[c], 1)
                    if what == "turn":
                        n, s = arg, arg % 2
                        count = turn5(kk) if n == SLOTS - 1 else nth(kk, TURN, n + 2)
                        pe.wait_ge(turn_drained, count - 1)
                        for c in range(KC):
                            pe.wait_ge(h_ready[c], nth(kk, 6, n))
                        o = bank3(turn_bank, GS)
                        for g in range(GS):
                            for c in range(KC):
                                last = pe.transpose(o[:, g, c * P:(c + 1) * P], h_feat[s][:, c, g * P:(g + 1) * P], ident[:])
                        last.then_inc(turn_filled, 1)
                    if what == "att" and arg[2] == 0:
                        s, j, _ = arg
                        if j or not (isinstance(kk, int) and kk == 0):
                            pe.wait_ge(att_drained[s], kk * NJ + j)
                            if j == 0:
                                pe.nop(nofuse=True)
                        content(s, kk, *CONTENT[j]).then_inc(att_filled[s], 1)

            def content(s, kg, layer, kind, u):
                bank = att_bank[s]
                if kind == "T" and layer == 1:
                    pe.wait_ge(y0n_ready[s], nth(kg, 1, 0))
                    return turn(bank, y0[s])
                if kind == "T":
                    pe.wait_ge(xn_ready[s], nth(kg, 2, layer - 2))
                    return turn(bank, xn[s])
                if kind == "P":
                    w_hi, w_lo, w = {1: (p1_hi, p1_lo, L1C), 2: (p2_hi, p2_lo, L2C), 3: (p3_hi, p3_lo, L2C)}[layer]
                    for kc in range(KC):
                        a_hi, a_lo = (t[s][:, kc, u * P:(u + 1) * P] for t in (xT_hi, xT_lo))
                        last = three_pass(bank[:, 0:w], a_hi, a_lo, w_hi[:, kc, :], w_lo[:, kc, :],
                                          start=(kc == 0), stop=(kc == KC - 1))
                    return last
                if kind == "R":
                    pe.wait_ge(parts_ready[s], nth(kg, 3, layer - 1))
                    pe.nop(nofuse=True)
                    w = 48 if layer == 1 else 6
                    src = parts[s] if layer == 1 else parts2[s]
                    o = bank[0:w, 0:P].bitcast(BF16).rearrange("r (g i) -> r g i", g=GS)
                    for g in range(GS):
                        last = pe.transpose(o[:, g, :], src[:, g].rearrange("p a b -> p (a b)"), ident_b[:])
                    return last
                if kind == "X" and layer == 1:
                    pe.wait_ge(neg_moved[s], nth(kg, 2, 1))
                    g, half = divmod(u, 2)
                    row = rows[s][0:48, g, :]
                    pe.matmul(bank[:], ident_b[:], neg1[s][:, g, :].unsqueeze(1).to_broadcast([P, 4, P]),
                              start=True, stop=False, skip_group_check=True)
                    pe.matmul(bank[:], row, sel16[:, 4 * half:4 * half + 4, :].rearrange("r a b -> r (a b)"),
                              start=False, stop=False, skip_group_check=True)
                    for q in range(4):
                        last = pe.matmul(bank[:, q * P:(q + 1) * P], sel16[:, H + 4 * half + q, :], row,
                                         start=False, stop=(q == 3), skip_group_check=True)
                    return last
                if kind == "X":
                    pe.wait_ge(neg_moved[s], nth(kg, 2, 1))
                    for g in range(GS):
                        o = bank[:, g * P:(g + 1) * P]
                        row = rows[s][0:6, g, :]
                        if layer == 2:
                            pe.matmul(o, neg3[s][:, g, :], ident_b[:], start=(g == 0), stop=False, skip_group_check=True)
                        else:
                            pe.matmul(o, ident_b[:], neg3[s][:, g, :], start=(g == 0), stop=False, skip_group_check=True)
                        free, part = (0, 1) if layer == 2 else (1, 0)
                        pe.matmul(o, sel2[:, free, :], row, start=False, stop=False, skip_group_check=True)
                        last = pe.matmul(o, row, sel2[:, part, :], start=False, stop=(g == 1), skip_group_check=True)
                    return last
                if kind == "Y":
                    if layer == 1:
                        pe.wait_ge(prob_ready[s], nth(kg, 5, u))
                        for q in range(4):
                            last = pe.transpose(bank[:, q * P:(q + 1) * P], prob[s][u % 2][:, q, :], ident[:])
                    else:
                        pe.wait_ge(summed[s], nth(kg, 2, 1))
                        for g in range(GS):
                            last = pe.transpose(bank[:, g * P:(g + 1) * P], prob[s][0][:, g, :], ident[:])
                    return last
                if layer == 1:
                    for q in range(H):
                        last = pe.matmul(bank[:, q * (C + 1):(q + 1) * (C + 1)], probT[s][:, q, :],
                                         h1[s][:, u, q, :], start=True, stop=True)
                    return last
                if layer == 2:
                    pe.wait_ge(prob_ready[s], nth(kg, 5, 4))
                for g in range(GS):
                    lhs = prob[s][0][:, g, :] if layer == 2 else probT[s][:, g, :]
                    last = pe.matmul(bank[:, g * D:(g + 1) * D], lhs, h2[s][:, g, 0:D], start=True, stop=True)
                return last

            body(0, True, False)
            with pe.Fori(1, NB - 1) as k:
                body(k, True, True)
            body(NB - 1, True, True, more=False)
            body(NB, False, True)

        @block.scalar
        def _(act):
            for q, (what, m, i) in enumerate(panels):
                if copied(panels[q]):
                    bank = setup_bank[q % len(setup_bank)]
                    act.wait_ge(setup_filled, q + 1)
                    to = {"ih": wihT, "w": wT, "p1": p1T, "p2": p2T}[m]
                    to = to[:, i] if m == "w" else to[:]
                    to = to.rearrange("p k e -> p (k e)")
                    if m == "ih":
                        to = to[:, i * 512:(i + 1) * 512]
                    act.activation(to, bank[:], ACT.Copy).then_inc(setup_copied, 1)

            def body(k, gru, att, more=True):
                for part in (order if gru else last_order)["act"]:
                    what, arg, kk, on = part_of(part, k, gru, att, more)
                    if not on:
                        continue
                    if what == "init":
                        init(arg, kk)
                    if what == "agg":
                        act.wait_ge(agg_filled, nth(kk, 6, arg))
                        act.activation(flat(u_hi), agg_bank[:], ACT.Copy).then_inc(u_hi_ready, 1)
                    if what == "gates_u" and arg[2] == 2:
                        n, c, _ = arg
                        act.wait_ge(gates_filled[c], nth(kk, 6, n))
                        act.activation(tr[c][:], bank3(gates_rz[c], 2)[:, 0, :], ACT.Tanh,
                                       bias=half_b[:, c:c + 1], scale=0.5)
                        act.activation(hn[c][:], bank3(gates_ih[c], 2)[:, 1, :], ACT.Identity,
                                       bias=half_bh[:, 4 + c:5 + c], scale=0.5).then_inc(r_hn_ready[c], 1)
                        act.wait_ge(e_ready[c], kk * 6 + n)
                        act.activation(tz[c][:], bank3(gates_rz[c], 2)[:, 1, :], ACT.Tanh,
                                       bias=half_b[:, KC + c:KC + c + 1], scale=0.5).then_inc(z_ready[c], 1)
                    if what == "gru":
                        n, c = arg
                        act.wait_ge(pre_ready[c], nth(kk, 6, n))
                        act.activation(nn[c][:], pre[c][:], ACT.Tanh, bias=bi[:, 4 + c:5 + c]).then_inc(n_ready[c], 1)
                    if what == "turn" and arg < SLOTS - NS:
                        act.wait_ge(turn_filled, nth(kk, TURN, arg + 2))
                        act.activation(flat(h_node[arg % 2]), turn_bank[:], ACT.Copy).then_inc(turn_drained, 1)
                    if what == "norm0b":
                        norm_apply(arg, kk, 0, y0[arg])
                    if what == "att":
                        attend(*arg[:2], kk, *CONTENT[arg[1]], arg[2])

            def attend(s, j, kg, layer, kind, u, phase):
                bank = att_bank[s]
                if phase == 0 and (kind in "TRX" or (kind == "P" and layer > 1) or kind == "Y"):
                    act.wait_ge(att_filled[s], nth(kg, NJ, j))
                if phase == 0 and kind == "T":
                    act.activation(flat(xT_hi[s]), bank[:], ACT.Copy).then_inc(xT_hi_ready[s], 1)
                if phase == 0 and kind == "P" and layer > 1:
                    act.activation(h2[s][:, u, :], bank[:, 0:L2C], ACT.Copy).then_inc(att_drained[s], 1)
                if phase == 0 and kind == "R":
                    w = 48 if layer == 1 else 6
                    act.activation(flat(rows[s][0:w]), bank[0:w, 0:P].bitcast(BF16), ACT.Copy).then_inc(att_drained[s], 1)
                if phase == 0 and kind == "X":
                    w = 4 if layer == 1 else GS
                    e = flat(prob[s][u % 2][:, 0:w, :])
                    act.activation(e, bank[:, 0:w * P], ACT.Copy, scale=-SLOPE).then_inc(scaled_ready[s], 1)
                if phase == 0 and kind == "Y":
                    w = 4 if layer == 1 else GS
                    q = 4 * (u % 2)
                    act.activation(flat(probT[s][:, q:q + w, :]), bank[:, 0:w * P], ACT.Copy).then_inc(att_drained[s], 1)
                if phase == 1 and kind == "X" and layer == 1:
                    act.wait_ge(mtop_ready[s], nth(kg, 6, u))
                    for q in range(4):
                        e = prob[s][u % 2][:, q, :]
                        last = act.activation(e, e, ACT.Exp, scale=-1.0, bias=mtop[s][u % 2][:, q:q + 1])
                    last.then_inc(prob_ready[s], 1)
                if phase == 1 and kind == "X" and layer > 1:
                    act.wait_ge(mtop_ready[s], nth(kg, 6, 2 + layer))
                    for g in range(GS):
                        last = act.activation(prob[s][0][:, g, :], prob[s][0][:, g, :], ACT.Exp, scale=-1.0,
                                              bias=mtop[s][0][:, g:g + 1], accum_out=zsum[s][:, g:g + 1])
                    last.then_inc(summed[s], 1)
                if phase == 1 and kind == "A" and layer == 2:
                    act.wait_ge(below_ready[s], nth(kg, 1, 0))
                    act.activation(below[s][:], below[s][:], ACT.Exp).then_inc(elu_ready[s], 1)
                if kind == "A" and (layer, phase) in ((1, 1), (2, 3), (3, 1)):
                    norm_apply(s, kg, layer, y[s])

            def norm_apply(s, kg, i, src):
                w, count = norm(kg, i)
                act.wait_ge(shift_ready[w][s], count)
                if i == 3:
                    act.wait_ge(stored[s], 16 * kg + 1)
                to, ready = ((y0, y0n_ready), (xn, xn_ready), (xn, xn_ready), (result, result_ready))[i]
                for g in range(GS):
                    last = act.activation(to[s][:, g, :], src[:, g, :], ACT.Identity,
                                          bias=shift[w][s][:, g:g + 1], scale=rstd[w][s][:, g:g + 1])
                last.then_inc(ready[s], 1)

            def init(s, k):
                act.wait_ge(turn_filled, init_turn(s, k))
                act.activation(flat(h_hi[s]), turn_bank[:], ACT.Copy)
                act.activation(flat(h_feat[s]), turn_bank[:], ACT.Copy).then_inc(x_split[s], 1)

            def start():
                init(0, 0)

            start()
            act.wait_ge(setup_done, 1)
            body(0, True, False)
            with act.Fori(1, NB - 1) as k:
                body(k, True, True)
            body(NB - 1, True, True, more=False)
            body(NB, False, True)

        @block.vector
        def _(dve):
            dve.memset(a_block[:], 0.0).then_inc(block_zero, 1)
            for s in range(NS):
                last = dve.memset(h1[s][:], 1.0)
            last.then_inc(setup_dve, 1)
            dve.wait_ge(ident_ready, 1)
            dve.tensor_copy(ident_b[:], ident[:]).then_inc(setup_dve, 1)
            dve.tensor_tensor(pick16[:], ident[0:48, 0:16], ident[0:48, 16:32], ALU.add)
            dve.tensor_tensor(pick2[:], ident[0:6, 0:2], ident[0:6, 2:4], ALU.add).then_inc(setup_dve, 1)
            dve.wait_ge(setup_dve, 3)
            dve.tensor_tensor(pick16[:], pick16[:], ident[0:48, 32:48], ALU.add)
            dve.tensor_tensor(pick2[:], pick2[:], ident[0:6, 4:6], ALU.add).then_inc(setup_dve, 1)
            dve.wait_ge(setup_dve, 4)
            dve.tensor_copy(sel16[:], pick16[:].unsqueeze(2).to_broadcast([48, 16, P]))
            dve.tensor_copy(sel2[:], pick2[:].unsqueeze(2).to_broadcast([6, 2, P]))

            def two_parts(hi, lo, src, n):
                dve.tensor_copy(hi, src).then_inc(setup_hi, 1)
                dve.wait_ge(setup_hi, n)
                return dve.tensor_tensor(lo, src, hi.bitcast(F32), ALU.subtract)

            pairs = 0
            for q, (what, m, i) in enumerate(panels):
                if copied(panels[q]):
                    continue
                if q == FIRST_FOLD:
                    for m1, hi, lo, raw in (("p1", p1_hi, p1_lo, raw_p1), ("p2", p2_hi, p2_lo, raw_p2)):
                        pairs += 1
                        dve.wait_ge(weight_in[m1], 16)
                        two_parts(hi[:, :, 0:D], lo[:, :, 0:D], raw[:], pairs)
                if q == FIRST_TERMS:
                    dve.wait_ge(vectors_in, 16 * N_VECTORS)
                    dve.tensor_copy(b_wide[:], b_col[:].unsqueeze(2).to_broadcast([P, KC, P])).then_inc(setup_dve, 1)
                    dve.tensor_tensor(bsum[:], bi[:], bh[:], ALU.add).then_inc(setup_dve, 1)
                    dve.tensor_scalar(half_bh[:], bh[:], 0.5, None, ALU.mult)
                    dve.wait_ge(setup_dve, 6)
                    dve.tensor_scalar(half_b[:], bsum[:], 0.5, None, ALU.mult)
                bank = setup_bank[q % len(setup_bank)]
                dve.wait_ge(setup_filled, q + 1)
                if what == "turn" and m == "hh":
                    hi, lo = (t[:].rearrange("p k e -> p (k e)")[:, i * 512:(i + 1) * 512] for t in (whh_hi, whh_lo))
                    src = bank[:]
                elif what == "turn":
                    hi, lo, src = p3_hi[:, :, 0:D], p3_lo[:, :, 0:D], bank3(bank, KC)
                elif what == "fold":
                    dc, nh = i
                    n0, n1 = ((0, 512), (512, G3))[nh]
                    hi, lo, src = wc_hi[:, m, dc, n0:n1], wc_lo[:, m, dc, n0:n1], bank[:, 0:n1 - n0]
                elif m == "bias":
                    dve.tensor_copy(bias1[:, D:L1C], bank[:, 0:2 * H]).then_inc(setup_split, 1)
                    continue
                else:
                    hi, lo, w = {"p1": (p1_hi, p1_lo, L1C), "p2": (p2_hi, p2_lo, L2C), "p3": (p3_hi, p3_lo, L2C)}[m]
                    hi, lo, src = hi[:, i, D:w], lo[:, i, D:w], bank[:, 0:w - D]
                pairs += 1
                two_parts(hi, lo, src, pairs).then_inc(setup_split, 1)
            dve.wait_ge(*emptied(len(panels) - 1))
            dve.nop(nofuse=True).then_inc(setup_done, 1)

            def norm_stats(s, kg, i, src):
                w, count = norm(kg, i)
                if i == 0:
                    dve.wait_ge(turn_drained, y0_count(s, kg))
                elif i == 3:
                    dve.wait_ge(att_drained[s], nth(kg, NJ, NJ - 1))
                else:
                    dve.wait_ge(y_ready[s], nth(kg, 2, i - 1))
                for g in range(GS):
                    last = dve.bn_stats(stats[w][s][:, g, :], src[:, g, :])
                last.then_inc(stats_ready[w][s], 1)
                dve.wait_ge(stats_ready[w][s], count)
                dve.nop(nofuse=True)
                for g in range(GS):
                    last = dve.bn_aggr(mv[w][s][:, g, :], stats[w][s][:, g, :])
                last.then_inc(mv_ready[w][s], 1)
                dve.wait_ge(mv_ready[w][s], count)
                dve.tensor_scalar(minus_mean[w][s][:], mv[w][s][:, :, 0], -1.0, None, ALU.mult)
                dve.tensor_scalar(veps[w][s][:], mv[w][s][:, :, 1], EPS, None, ALU.add).then_inc(veps_ready[w][s], 1)

            def body(k, gru, att, more=True):
                for part in (order if gru else last_order)["dve"]:
                    what, arg, kk, on = part_of(part, k, gru, att, more)
                    if not on:
                        continue
                    if what == "edges":
                        find_edges(arg, kk)
                    if what == "init":
                        init(arg, kk)
                    if what == "negs":
                        s = arg
                        dve.wait_ge(adj_loaded[s], 16 * (kk + 1))
                        dve.wait_ge(neg_moved[s], kk * 2)
                        dve.tensor_scalar(neg1_next[s][:], adj_in[s][:], 1, MASKED, ALU.not_equal, ALU.mult).then_inc(negs_ready[s], 1)
                        dve.tensor_scalar(neg3_next[s][:], adj_in[s][:], 0, MASKED, ALU.is_le, ALU.mult).then_inc(negs_ready[s], 1)
                    if what == "norm0":
                        norm_stats(arg, kk, 0, y0[arg])
                    if what == "agg":
                        dve.wait_ge(u_hi_ready, nth(kk, 6, arg))
                        dve.tensor_tensor(flat(u_lo), agg_bank[:], flat(u_hi).bitcast(F32), ALU.subtract).then_inc(u_ready, 1)
                    if what == "gates_u" and arg[2] == 2:
                        n, c, _ = arg
                        dve.wait_ge(r_hn_ready[c], nth(kk, 6, n))
                        dve.scalar_tensor_tensor(pre[c][:], tr[c][:], 1.0, hn[c][:], ALU.add, ALU.mult).then_inc(q_ready[c], 1)
                        dve.wait_ge(q_ready[c], nth(kk, 6, n))
                        dve.tensor_tensor(pre[c][:], bank3(gates_ih[c], 2)[:, 0, :], pre[c][:], ALU.add).then_inc(pre_ready[c], 1)
                    if what == "gru":
                        n, c = arg
                        s = n % 2
                        dve.wait_ge(d_ready[c], nth(kk, 6, n))
                        dve.wait_ge(z_ready[c], nth(kk, 6, n))
                        dve.scalar_tensor_tensor(dd[c][:], tz[c][:], 1.0, dd[c][:], ALU.add, ALU.mult).then_inc(e_ready[c], 1)
                        dve.wait_ge(e_ready[c], nth(kk, 6, n))
                        dve.scalar_tensor_tensor(h_feat[s][:, c, :], dd[c][:], 0.5, nn[c][:], ALU.mult, ALU.add).then_inc(h_ready[c], 1)
                    if what == "turn" and arg >= SLOTS - NS:
                        s = arg % 2
                        dve.wait_ge(turn_filled, y0_count(s, kk))
                        dve.tensor_tensor(flat(y0[s]), turn_bank[:], flat(x_keep[s]), ALU.add).then_inc(turn_drained, 1)
                    if what == "att":
                        s, j, phase = arg
                        (attend if phase == 0 else attend_later)(s, kk, j, *CONTENT[j], phase)

            def find_edges(s, k):
                dve.wait_ge(adj_loaded[s], 16 * (k + 1))
                dve.tensor_scalar(edges[s][:], adj_in[s][:], 0, None, ALU.not_equal).then_inc(edges_ready[s], 1)

            def init(s, k):
                dve.wait_ge(x_split[s], nth(k, 1, 0))
                dve.tensor_tensor(flat(h_lo[s]), turn_bank[:], flat(h_hi[s]).bitcast(F32), ALU.subtract).then_inc(turn_drained, 1)

            def start():
                find_edges(0, 0)
                init(0, 0)

            def attend(s, kg, j, layer, kind, u, phase):
                bank = att_bank[s]
                filled = nth(kg, NJ, j)
                if kind == "T":
                    dve.wait_ge(xT_hi_ready[s], nth(kg, 3, layer - 1))
                    dve.tensor_tensor(xT_lo[s][:].rearrange("p c t -> p (c t)"), bank[:],
                                      xT_hi[s][:].rearrange("p c t -> p (c t)").bitcast(F32), ALU.subtract).then_inc(att_drained[s], 1)
                if kind == "P" and layer == 1:
                    dve.wait_ge(att_filled[s], filled)
                    dve.tensor_tensor(h1[s][:, u, :, 0:C], bank[:, 0:D].rearrange("p (h c) -> p h c", h=H),
                                      bias1[:, 0:D].rearrange("p (h c) -> p h c", h=H), ALU.add)
                    last = dve.tensor_tensor(terms[s][:, u, :], bank[:, D:L1C], bias1[:, D:L1C], ALU.add)
                    last.then_inc(att_drained[s], 1)
                if kind == "X":
                    w = 4 if layer == 1 else GS
                    i = u if layer == 1 else 2 + layer
                    e = prob[s][u % 2][:, 0:w, :]
                    b = bank[:, 0:w * P].rearrange("p (a b) -> p a b", a=w)
                    dve.wait_ge(scaled_ready[s], nth(kg, 6, i))
                    dve.scalar_tensor_tensor(e, b, -1.0, e, ALU.mult, ALU.min).then_inc(att_drained[s], 1)
                    dve.wait_ge(att_drained[s], filled)
                    dve.tensor_reduce(mtop[s][u % 2][:, 0:w], e, AX.X, ALU.min).then_inc(mtop_ready[s], 1)
                if kind == "A" and layer == 1:
                    dve.wait_ge(att_filled[s], filled)
                    o = bank[:, 0:H * (C + 1)].rearrange("p (h c) -> p h c", h=H)
                    dve.reciprocal(rz[s][:], o[:, :, C]).then_inc(rz_ready[s], 1)
                    dve.wait_ge(rz_ready[s], nth(kg, 4, u))
                    dve.tensor_tensor(y[s][:, u].rearrange("p (h c) -> p h c", h=H), o[:, :, 0:C],
                                      rz[s][:].unsqueeze(2).to_broadcast([P, H, C]), ALU.mult).then_inc(att_drained[s], 1)
                    if u == 1:
                        dve.wait_ge(att_drained[s], filled)
                        dve.tensor_tensor(y[s][:], y[s][:], y0[s][:], ALU.add).then_inc(y_ready[s], 1)
                        norm_stats(s, kg, 1, y[s])
                if kind == "A" and layer == 2:
                    dve.wait_ge(att_filled[s], filled)
                    dve.tensor_scalar(below[s][:].rearrange("p g d -> p (g d)"), bank[:], 0.0, None, ALU.min).then_inc(below_ready[s], 1)
                if kind == "A" and layer == 3:
                    dve.wait_ge(att_filled[s], filled)
                    dve.wait_ge(rz_ready[s], nth(kg, 4, 3))
                    for g in range(GS):
                        last = dve.scalar_tensor_tensor(y[s][:, g, :], bank[:, g * D:(g + 1) * D], rz[s][:, g:g + 1],
                                                        xn[s][:, g, :], ALU.mult, ALU.add)
                    last.then_inc(att_drained[s], 1)
                    norm_stats(s, kg, 3, y[s])

            def attend_later(s, kg, j, layer, kind, u, phase):
                bank = att_bank[s]
                if kind == "X" and layer > 1 and phase == 2:
                    dve.wait_ge(summed[s], nth(kg, 2, layer - 2))
                    dve.reciprocal(rz[s][:, 0:GS], zsum[s][:]).then_inc(rz_ready[s], 1)
                    if layer == 2:
                        dve.wait_ge(rz_ready[s], nth(kg, 4, 2))
                        for g in range(GS):
                            last = dve.tensor_scalar(prob[s][0][:, g, :], prob[s][0][:, g, :], rz[s][:, g:g + 1], None, ALU.mult)
                        last.then_inc(prob_ready[s], 1)
                if kind == "A" and (layer, phase) == (2, 2):
                    dve.wait_ge(elu_ready[s], nth(kg, 1, 0))
                    dve.scalar_tensor_tensor(flat(below[s]), bank[:], 0.0, flat(below[s]), ALU.max, ALU.add).then_inc(att_drained[s], 1)
                    dve.wait_ge(att_drained[s], nth(kg, NJ, j))
                    dve.scalar_tensor_tensor(y[s][:], below[s][:], -1.0, xn[s][:], ALU.add, ALU.add).then_inc(y_ready[s], 1)
                    norm_stats(s, kg, 2, y[s])

            start()
            body(0, True, False)
            with dve.Fori(1, NB - 1) as k:
                body(k, True, True)
            body(NB - 1, True, True, more=False)
            body(NB, False, True)


_INS = ["x", "adj", "L0_gnn_weight", "L0_gnn_w_ih", "L0_gnn_w_hh", "L0_gnn_b_ih", "L0_gnn_b_hh", "L1_gnn_proj_kernel",
        "L1_gnn_proj_bias", "L1_gnn_attn_fst", "L1_gnn_attn_snd", "L2_gnn_W", "L2_gnn_a", "L3_gnn_W", "L3_gnn_a"]


def kernel(**inputs):
    import numpy as _np
    import concourse.bacc as _bacc
    from concourse import mybir as _mybir
    from concourse.bass_utils import run_bass_kernel_spmd as _run

    nc = _bacc.Bacc("TRN2", target_bir_lowering=False, num_devices=1)
    arrays, args = {}, []
    for name in _INS:
        a = _np.ascontiguousarray(inputs[name])
        arrays[f"in_{name}"] = a
        args.append(nc.dram_tensor(f"in_{name}", a.shape, _mybir.dt.from_np(a.dtype), kind="ExternalInput").ap())
    shape = arrays["in_x"].shape
    args.append(nc.dram_tensor("out_0", shape, _mybir.dt.float32, kind="ExternalOutput").ap())
    graph_layers(nc, *args)
    r = _run(nc, [arrays], core_ids=[0])
    return r.results[0]["out_0"]
```
